# Optimizing a Trainium2 kernel written in Bass

```python
import numpy as np
import jax
import jax.numpy as jnp

def _softmax(x, axis=-1):
    return jax.nn.softmax(x, axis=axis)

def _gelu(x):
    return jax.nn.gelu(x, approximate=True)

def _silu(x):
    return jax.nn.silu(x)

def _sigmoid(x):
    return jax.nn.sigmoid(x)

def _layernorm(x, axis=-1, eps=1e-05):
    m = jnp.mean(x, axis=axis, keepdims=True)
    v = jnp.var(x, axis=axis, keepdims=True)
    return (x - m) / jnp.sqrt(v + eps)

def _scatter_add(tgt, idx, src, axis=0):
    return tgt.at[idx].add(src)

def _segment_sum(src, seg, n):
    return jax.ops.segment_sum(src, seg, n)
kernel_name = 'mk_adj_resnorm_d4_adj_r2_c570d3'

def setup_inputs(seed: int=0):
    np.random.seed(seed)
    _w = jnp.asarray

    def _rec_inputs():
        import jax
        import jax.numpy as jnp
        _gk = jax.random.key(seed)
        x = -0.0003929 + 0.9999 * jax.random.normal(jax.random.fold_in(_gk, 1), (128, 128, 256), jnp.float32)
        _a = jax.random.bernoulli(jax.random.fold_in(_gk, 2), 0.03125, (128, 128, 128))
        _a = jnp.logical_or(_a, jnp.swapaxes(_a, -1, -2))
        _a = jnp.logical_or(_a, jnp.eye(128, dtype=bool))
        _af = _a.astype(jnp.float32)
        _af = _af * jax.random.uniform(jax.random.fold_in(_gk, 3), (128, 128, 128), jnp.float32, 0.05, 1)
        adj = _af
        return (x, adj)
    x, adj = _rec_inputs()

    def _L0_gnn_setup():
        import jax, jax.numpy as jnp
        import numpy as np
        B, N, F_IN, F_HID, F_OUT = (32, 512, 256, 256, 256)

        def _gcn_layer(x, adj, W, b):
            support = jnp.einsum('bnf,fh->bnh', x, W)
            return jnp.einsum('bnm,bmh->bnh', adj, support) + b
        key = jax.random.key(seed)
        ks = jax.random.split(key, 8)

        def xavier(k, fan_in, fan_out):
            bound = float(np.sqrt(6.0 / (fan_in + fan_out)))
            return jax.random.uniform(k, (fan_in, fan_out), jnp.float32, -bound, bound)
        return {'batch_graph': jax.random.normal(ks[0], (B, N, F_IN), jnp.float32), 'adj': jax.random.uniform(ks[1], (B, N, N), jnp.float32), 'W1': xavier(ks[2], F_IN, F_HID), 'b1': jnp.zeros((F_HID,), jnp.float32), 'W2': xavier(ks[3], F_HID, F_HID), 'b2': jnp.zeros((F_HID,), jnp.float32), 'W3': xavier(ks[4], F_HID, F_OUT), 'b3': jnp.zeros((F_OUT,), jnp.float32)}
    _L0_gnn_all = _L0_gnn_setup()
    _L0_gnn_in = {k: v for k, v in _L0_gnn_all.items() if k in ('W1', 'b1', 'W2', 'b2', 'W3', 'b3')}
    del _L0_gnn_all

    def _L1_gnn_setup():
        import jax, jax.numpy as jnp
        import numpy as np
        EPS_LN = 1e-05

        def hypergraph_conv(x, adj, W, b):
            N, C, _ = adj.shape
            H = (adj != 0).astype(x.dtype)
            w = adj.reshape(N, -1)[:, :C]
            xw = jnp.einsum('ncd,hd->nch', x, W)
            Dn = jnp.einsum('nce,ne->nc', H, w)
            Dn = jnp.where(Dn > 0, 1.0 / Dn, 0.0)
            Be = H.sum(axis=1)
            Be = jnp.where(Be > 0, 1.0 / Be, 0.0)
            m = Be[:, :, None] * jnp.einsum('nce,nch->neh', H, xw)
            out = Dn[:, :, None] * jnp.einsum('nce,neh->nch', H, m)
            return out + b

        def layer_norm(x, g, b):
            mu = jnp.mean(x, axis=-1, keepdims=True)
            var = jnp.var(x, axis=-1, keepdims=True)
            return (x - mu) * jax.lax.rsqrt(var + EPS_LN) * g + b
        key = jax.random.key(seed)
        ks = jax.random.split(key, 4)
        N, C, Din, Dh, Dout = (16, 512, 256, 512, 256)
        x = jax.random.normal(ks[0], (N, C, Din), dtype=jnp.float32)
        adj = jax.random.uniform(ks[1], (N, C, C), dtype=jnp.float32, minval=0.1, maxval=1.0)
        W1 = jax.random.normal(ks[2], (Dh, Din), dtype=jnp.float32) * (1.0 / np.sqrt(Din))
        b1 = jnp.zeros((Dh,), dtype=jnp.float32)
        gamma = jnp.ones((Dh,), dtype=jnp.float32)
        beta = jnp.zeros((Dh,), dtype=jnp.float32)
        W2 = jax.random.normal(ks[3], (Dout, Dh), dtype=jnp.float32) * (1.0 / np.sqrt(Dh))
        b2 = jnp.zeros((Dout,), dtype=jnp.float32)
        return {'x': x, 'adj': adj, 'W1': W1, 'b1': b1, 'gamma': gamma, 'beta': beta, 'W2': W2, 'b2': b2}
    _L1_gnn_all = _L1_gnn_setup()
    _L1_gnn_in = {k: v for k, v in _L1_gnn_all.items() if k in ('W1', 'b1', 'gamma', 'beta', 'W2', 'b2')}
    del _L1_gnn_all

    def _L2_gnn_setup():
        import jax, jax.numpy as jnp
        import numpy as np
        IN_DIM = 256
        ATT_DIM = 64
        B, N = (4, 2048)
        key = jax.random.key(seed)
        k1, k2, k3, k4 = jax.random.split(key, 4)
        x = jax.random.normal(k1, (B, N, IN_DIM), dtype=jnp.float32)
        adj_matrix = (jax.random.uniform(k2, (B, N, N)) < 0.05).astype(jnp.float32)
        W_qk = jax.random.normal(k3, (2 * ATT_DIM, IN_DIM), dtype=jnp.float32) / np.sqrt(IN_DIM)
        W_v = jax.random.normal(k4, (IN_DIM, IN_DIM), dtype=jnp.float32) / np.sqrt(IN_DIM)
        return {'x': x, 'adj_matrix': adj_matrix, 'W_qk': W_qk, 'W_v': W_v}
    _L2_gnn_all = _L2_gnn_setup()
    _L2_gnn_in = {k: v for k, v in _L2_gnn_all.items() if k in ('W_qk', 'W_v')}
    del _L2_gnn_all

    def _L3_gnn_setup():
        import jax, jax.numpy as jnp
        import numpy as np
        B, N, DIN, DOUT, K = (4, 1024, 256, 256, 3)
        key = jax.random.key(seed)
        ks = jax.random.split(key, 8)
        X = jax.random.normal(ks[0], (B, N, DIN), dtype=jnp.float32)
        A = jax.random.uniform(ks[1], (B, N, N), dtype=jnp.float32)
        Wv = jax.random.normal(ks[2], (DIN, DOUT), dtype=jnp.float32) * 0.02
        bv = jax.random.normal(ks[3], (DOUT,), dtype=jnp.float32) * 0.02
        aw = jax.random.normal(ks[4], (2 * DOUT, 1), dtype=jnp.float32) * 0.05
        ab = jax.random.normal(ks[5], (1,), dtype=jnp.float32) * 0.05
        Wk = jax.random.normal(ks[6], (K, DIN, DOUT), dtype=jnp.float32) * 0.02
        bk = jax.random.normal(ks[7], (K, DOUT), dtype=jnp.float32) * 0.02
        return {'X': X, 'A': A, 'Wv': Wv, 'bv': bv, 'aw': aw, 'ab': ab, 'Wk': Wk, 'bk': bk}
    _L3_gnn_all = _L3_gnn_setup()
    _L3_gnn_in = {k: v for k, v in _L3_gnn_all.items() if k in ('Wv', 'bv', 'aw', 'ab', 'Wk', 'bk')}
    del _L3_gnn_all
    return {'x': x, 'adj': adj, 'L0_gnn_W1': _L0_gnn_in['W1'], 'L0_gnn_b1': _L0_gnn_in['b1'], 'L0_gnn_W2': _L0_gnn_in['W2'], 'L0_gnn_b2': _L0_gnn_in['b2'], 'L0_gnn_W3': _L0_gnn_in['W3'], 'L0_gnn_b3': _L0_gnn_in['b3'], 'L1_gnn_W1': _L1_gnn_in['W1'], 'L1_gnn_b1': _L1_gnn_in['b1'], 'L1_gnn_gamma': _L1_gnn_in['gamma'], 'L1_gnn_beta': _L1_gnn_in['beta'], 'L1_gnn_W2': _L1_gnn_in['W2'], 'L1_gnn_b2': _L1_gnn_in['b2'], 'L2_gnn_W_qk': _L2_gnn_in['W_qk'], 'L2_gnn_W_v': _L2_gnn_in['W_v'], 'L3_gnn_Wv': _L3_gnn_in['Wv'], 'L3_gnn_bv': _L3_gnn_in['bv'], 'L3_gnn_aw': _L3_gnn_in['aw'], 'L3_gnn_ab': _L3_gnn_in['ab'], 'L3_gnn_Wk': _L3_gnn_in['Wk'], 'L3_gnn_bk': _L3_gnn_in['bk']}

def reference(x, adj, L0_gnn_W1, L0_gnn_b1, L0_gnn_W2, L0_gnn_b2, L0_gnn_W3, L0_gnn_b3, L1_gnn_W1, L1_gnn_b1, L1_gnn_gamma, L1_gnn_beta, L1_gnn_W2, L1_gnn_b2, L2_gnn_W_qk, L2_gnn_W_v, L3_gnn_Wv, L3_gnn_bv, L3_gnn_aw, L3_gnn_ab, L3_gnn_Wk, L3_gnn_bk):
    import jax
    import jax.numpy as jnp

    def _L0_gnn_ref(batch_graph, adj, W1, b1, W2, b2, W3, b3):
        import jax, jax.numpy as jnp
        import numpy as np
        B, N, F_IN, F_HID, F_OUT = (32, 512, 256, 256, 256)

        def _gcn_layer(x, adj, W, b):
            support = jnp.einsum('bnf,fh->bnh', x, W)
            return jnp.einsum('bnm,bmh->bnh', adj, support) + b
        x = jax.nn.relu(_gcn_layer(batch_graph, adj, W1, b1))
        x = jax.nn.relu(_gcn_layer(x, adj, W2, b2))
        out = _gcn_layer(x, adj, W3, b3)
        return out

    def _L1_gnn_ref(x, adj, W1, b1, gamma, beta, W2, b2):
        import jax, jax.numpy as jnp
        import numpy as np
        EPS_LN = 1e-05

        def hypergraph_conv(x, adj, W, b):
            N, C, _ = adj.shape
            H = (adj != 0).astype(x.dtype)
            w = adj.reshape(N, -1)[:, :C]
            xw = jnp.einsum('ncd,hd->nch', x, W)
            Dn = jnp.einsum('nce,ne->nc', H, w)
            Dn = jnp.where(Dn > 0, 1.0 / Dn, 0.0)
            Be = H.sum(axis=1)
            Be = jnp.where(Be > 0, 1.0 / Be, 0.0)
            m = Be[:, :, None] * jnp.einsum('nce,nch->neh', H, xw)
            out = Dn[:, :, None] * jnp.einsum('nce,neh->nch', H, m)
            return out + b

        def layer_norm(x, g, b):
            mu = jnp.mean(x, axis=-1, keepdims=True)
            var = jnp.var(x, axis=-1, keepdims=True)
            return (x - mu) * jax.lax.rsqrt(var + EPS_LN) * g + b
        h = jax.nn.relu(hypergraph_conv(x, adj, W1, b1))
        h = layer_norm(h, gamma, beta)
        y = hypergraph_conv(h, adj, W2, b2)
        return y + x

    def _L2_gnn_ref(x, adj_matrix, W_qk, W_v):
        import jax, jax.numpy as jnp
        import numpy as np
        IN_DIM = 256
        ATT_DIM = 64
        B, N = (4, 2048)
        qk = jnp.einsum('bnd,ed->bne', x, W_qk)
        q, k = jnp.split(qk, 2, axis=-1)
        v = jnp.einsum('bnd,ed->bne', x, W_v)
        inv_scale = 1.0 / ATT_DIM ** 0.5
        scores = jnp.einsum('bnd,bmd->bnm', q, k) * inv_scale
        w = jnp.sum(scores * adj_matrix, axis=-1, keepdims=True)
        w = jax.nn.softmax(w, axis=1)
        return w * v

    def _L3_gnn_ref(X, A, Wv, bv, aw, ab, Wk, bk):
        import jax, jax.numpy as jnp
        import numpy as np
        B, N, DIN, DOUT, K = (4, 1024, 256, 256, 3)
        d = Wv.shape[1]
        Xw = X @ Wv + bv
        sj = Xw @ aw[:d, 0]
        si = Xw @ aw[d:, 0]
        e = jax.nn.leaky_relu(sj[:, None, :] + si[:, :, None] + ab[0], negative_slope=0.2)
        alpha_matrix = A * jnp.exp(e)
        transition = alpha_matrix / (jnp.sum(alpha_matrix, axis=-1, keepdims=True) + 1e-12)
        H = jnp.zeros(X.shape[:-1] + (d,), dtype=X.dtype)
        Xk = X
        for k in range(Wk.shape[0]):
            H = H + Xk @ Wk[k] + bk[k]
            Xk = jnp.einsum('bij,bjd->bid', transition, Xk)
        return jax.nn.relu(H)
    x = _layernorm(x + _L0_gnn_ref(x, adj, L0_gnn_W1, L0_gnn_b1, L0_gnn_W2, L0_gnn_b2, L0_gnn_W3, L0_gnn_b3), axis=-1)
    x = _layernorm(x + _L1_gnn_ref(x, adj, L1_gnn_W1, L1_gnn_b1, L1_gnn_gamma, L1_gnn_beta, L1_gnn_W2, L1_gnn_b2), axis=-1)
    x = _layernorm(x + _L2_gnn_ref(x, adj, L2_gnn_W_qk, L2_gnn_W_v), axis=-1)
    x = _layernorm(x + _L3_gnn_ref(x, adj, L3_gnn_Wv, L3_gnn_bv, L3_gnn_aw, L3_gnn_ab, L3_gnn_Wk, L3_gnn_bk), axis=-1)
    return x

_drawn_inputs = setup_inputs


def setup_inputs(seed=0):
    import zlib

    import numpy as np

    out = dict(_drawn_inputs(seed))
    spreads = {'L0_gnn_b1': (0.0, 0.1),
     'L0_gnn_b2': (0.0, 0.317),
     'L0_gnn_b3': (0.0, 0.729),
     'L1_gnn_b1': (0.0, 0.1),
     'L1_gnn_gamma': (1.0, 0.2),
     'L1_gnn_beta': (0.0, 0.1),
     'L1_gnn_b2': (0.0, 0.1)}
    factors = {'L3_gnn_Wv': 6.374, 'L3_gnn_bv': 31.591, 'L3_gnn_aw': 2.991}
    for name, (base, spread) in spreads.items():
        noise = np.random.default_rng([zlib.crc32(name.encode()), seed]).standard_normal(out[name].shape)
        drawn = base * np.exp(spread * noise) if base else spread * noise
        out[name] = jnp.asarray(drawn.astype(out[name].dtype))
    for name, factor in factors.items():
        out[name] = (out[name] * factor).astype(out[name].dtype)
    return out
```

```python
from contextlib import ExitStack

import concourse.bass as bass
from concourse import mybir

ALU = mybir.AluOpType
ACT = mybir.ActivationFunctionType
AX = mybir.AxisListType
F32 = mybir.dt.float32

P = 128
EPS = 1e-5
TINY = 1.1754944e-38


class Signal:

    def __init__(self, sem, per_pair):
        self.sem, self.per = sem, per_pair

    def at(self, pair, k=None):
        return pair * self.per + (self.per if k is None else k)


def graph_block_kernel(
    nc, x, adj,
    gcn_w1, gcn_b1, gcn_w2, gcn_b2, gcn_w3, gcn_b3,
    hyp_w1, hyp_b1, hyp_gamma, hyp_beta, hyp_w2, hyp_b2,
    att_wqk, att_wv,
    dif_wv, dif_bv, dif_aw, dif_ab, dif_wk, dif_bk,
    out,
):
    B, N, F = x.shape
    G = 2
    PAIRS = B // G
    FC = F // P
    DH = hyp_w1.shape[0]
    HC = DH // P
    QK = att_wqk.shape[0]
    DA = QK // 2
    QKV = QK + F
    HOPS = dif_wk.shape[0]
    INV_SCALE = 1.0 / DA ** 0.5
    assert N == P and F == 2 * P and HC == 4 and HOPS == 3
    LAYERS = 4

    x_pairs = x.rearrange("(s g) n f -> s n g f", g=G)
    adj_pairs = adj.rearrange("(s g) n m -> s n g m", g=G)
    out_pairs = out.rearrange("(s g) n f -> s n g f", g=G)

    with ExitStack() as ctx:
        def sb(name, shape):
            return ctx.enter_context(nc.sbuf_tensor(name, shape, F32))

        def sem(name):
            return ctx.enter_context(nc.semaphore(name))

        def signal(name, per_pair=1):
            return Signal(sem(name), per_pair)

        ident = sb("ident", [P, P])
        ones = sb("ones", [P, 1])
        neg_half = sb("neg_half", [P, G])
        w1 = sb("w1", [P, FC, F])
        w2 = sb("w2", [P, FC, F])
        w3 = sb("w3", [P, FC, F])
        b1_col = sb("b1_col", [P, FC])
        b2_col = sb("b2_col", [P, FC])
        b3_rows = sb("b3_rows", [P, G, F])
        hyp_w1_nat = sb("hyp_w1_nat", [P, HC, F])
        hyp_w1T = sb("hyp_w1T", [P, FC, DH])
        hyp_b1_rows = sb("hyp_b1_rows", [P, DH])
        gamma_col = sb("gamma_col", [P, HC])
        beta_col = sb("beta_col", [P, HC])
        hyp_w2_nat = sb("hyp_w2_nat", [P, FC, DH])
        hyp_w2T = sb("hyp_w2T", [P, HC, F])
        hyp_w2g = sb("hyp_w2g", [P, HC, F])
        hyp_shift = sb("hyp_shift", [P, F])
        hyp_b2_rows = sb("hyp_b2_rows", [P, G, F])
        wqk_nat = sb("wqk_nat", [P, F])
        wv_nat = sb("wv_nat", [P, FC, F])
        w_qkv = sb("w_qkv", [P, FC, QKV])
        dif_wv_nat = sb("dif_wv_nat", [P, FC, F])
        dif_wvT = sb("dif_wvT", [P, FC, F])
        bv_col = sb("bv_col", [P, FC])
        aw_cols = sb("aw_cols", [P, 2, FC])
        ab_col = sb("ab_col", [P, 1])
        wa = sb("wa", [P, FC, 2])
        s_const = sb("s_const", [P, 1])
        s_part = sb("s_part", [P, 2])
        w_hop = sb("w_hop", [P, FC, HOPS, F])
        bk_rows = sb("bk_rows", [P, HOPS, F])
        bk_tmp = sb("bk_tmp", [P, F])
        bk_sum = sb("bk_sum", [P, G, F])

        x_in = sb("x_in", [P, G, F])
        adj_in = sb("adj_in", [P, G, N])
        adjT0 = sb("adjT0", [P, G, N])
        x_b3 = sb("x_b3", [P, G, F])
        axT = sb("axT", [P, FC, G, N])
        h1T = sb("h1T", [P, FC, G, N])
        s2 = sb("s2", [P, G, F])
        h2T = sb("h2T", [P, FC, G, N])
        s3 = sb("s3", [P, G, F])
        r0 = sb("r0", [P, G, F])
        x1 = sb("x1", [P, G, F])
        incT = sb("incT", [P, G, N])
        incT_w = sb("incT_w", [P, G, N])
        edge_size = sb("edge_size", [P, G])
        edge_size1 = sb("edge_size1", [P, G])
        edge_inv = sb("edge_inv", [P, G])
        deg_rhs = sb("deg_rhs", [P, G, 2])
        adjT1 = sb("adjT1", [P, G, N])
        kdeg = sb("kdeg", [P, G * N + G * 2])
        kmat = kdeg[:, 0:G * N].rearrange("p (g n) -> p g n", g=G)
        deg = kdeg[:, G * N:G * N + G * 2].rearrange("p (g j) -> p g j", g=G)
        deg_pos = sb("deg_pos", [P, G])
        deg_safe = sb("deg_safe", [P, G])
        deg_rec = sb("deg_rec", [P, G])
        deg_inv = sb("deg_inv", [P, G])
        row_sum = sb("row_sum", [P, G])
        kxT = sb("kxT", [P, FC, G, N])
        h_pre = sb("h_pre", [P, G, DH])
        h_act = sb("h_act", [P, G, DH])
        z = sb("z", [P, G, DH])
        kzT = sb("kzT", [P, G, HC, N])
        xx = sb("xx", [P, G, F])
        r1_base = sb("r1_base", [P, G, F])
        r1 = sb("r1", [P, G, F])
        x2 = sb("x2", [P, G, F])
        adjT2 = sb("adjT2", [P, G, N])
        x2T = sb("x2T", [P, FC, G, N])
        qkv = sb("qkv", [P, G, QKV])
        qak = sb("qak", [P, G, DA])
        score = sb("score", [P, G])
        neg_max = sb("neg_max", [G, 1])
        prob_e = sb("prob_e", [G, N])
        prob_sum = sb("prob_sum", [G, 1])
        prob_inv = sb("prob_inv", [G, 1])
        prob_row = sb("prob_row", [G, N])
        prob = sb("prob", [P, G])
        r2 = sb("r2", [P, G, F])
        x3 = sb("x3", [P, G, F])
        adjT3 = sb("adjT3", [P, G, N])
        x3T = sb("x3T", [P, FC, G, N])
        s_cols = sb("s_cols", [P, G, 2])
        s_col02 = sb("s_col02", [P, G])
        e_pos = sb("e_pos", [P, G, N])
        e_neg = sb("e_neg", [P, G, N])
        e_max = sb("e_max", [P, G, N])
        alphaT = sb("alphaT", [P, G, N])
        sum_eps = sb("sum_eps", [P, G])
        sum_inv = sb("sum_inv", [P, G])
        y0 = sb("y0", [P, G, F])
        y1 = sb("y1", [P, G, F])
        y2 = sb("y2", [P, G, F])
        hop1 = sb("hop1", [P, G, F])
        hop2 = sb("hop2", [P, G, F])
        x3_kept = sb("x3_kept", [P, G, F])
        r3 = sb("r3", [P, G, F])
        y_out = sb("y_out", [P, G, F])

        NORMS = ("ln0", "lnh", "ln1", "ln2", "ln3")
        stats = {n: sb(n + "_stats", [P, G, 6]) for n in NORMS}
        mean_gap = {n: sb(n + "_mean_gap", [P, G]) for n in NORMS}
        gap_square = {n: sb(n + "_gap_square", [P, G]) for n in NORMS}
        square_sum = {n: sb(n + "_square_sum", [P, G]) for n in NORMS}
        mean = {n: sb(n + "_mean", [P, G]) for n in NORMS}
        var_eps = {n: sb(n + "_var_eps", [P, G]) for n in NORMS}
        rstd = {n: sb(n + "_rstd", [P, G]) for n in NORMS}

        bank = [[ctx.enter_context(nc.psum_tensor(f"layer{l}_{b}", [P, 512], F32)) for b in range(2)]
                for l in range(LAYERS)]

        consts_in, ident_zero, ident_made, consts_set = map(sem, ("consts_in", "ident_zero", "ident_made", "consts_set"))
        weights_turned, weights_kept, shifts_made, bias_summed, setup_done = map(
            sem, ("weights_turned", "weights_kept", "shifts_made", "bias_summed", "setup_done"))
        x_loaded, adj_loaded, y_stored = signal("x_loaded", 16), signal("adj_loaded", 16), signal("y_stored", 16)
        adjT_ps, ax_ps, h1_ps, s2_ps, as2_ps, s3_ps, gcn_ps = (
            signal(n) for n in ("adjT_ps", "ax_ps", "h1_ps", "s2_ps", "as2_ps", "s3_ps", "gcn_ps"))
        k_ps, kx_ps, hyp2_ps = (signal(n) for n in ("k_ps", "kx_ps", "hyp2_ps"))
        hyp1_ps, kz_ps = signal("hyp1_ps", 2), signal("kz_ps", 2)
        x2T_ps, ak_ps, score_ps, prob_ps = (signal(n) for n in ("x2T_ps", "ak_ps", "score_ps", "prob_ps"))
        qkv_ps = signal("qkv_ps", 2)
        x3T_ps, s_ps, s_row_ps, y0_ps, sum_ps, hop1_ps, hop2_ps = (
            signal(n) for n in ("x3T_ps", "s_ps", "s_row_ps", "y0_ps", "sum_ps", "hop1_ps", "hop2_ps"))
        y12_ps = signal("y12_ps", 2)
        adjT_sb, ax_sb, s2_sb, s3_sb, k_sb, kx_sb, x2T_sb, x3T_sb = (
            signal(n) for n in ("adjT_sb", "ax_sb", "s2_sb", "s3_sb", "k_sb", "kx_sb", "x2T_sb", "x3T_sb"))
        h1_sb, h2_sb, kz_sb, qkv_sb, y12_sb, relu_sb = (
            signal(n, 2) for n in ("h1_sb", "h2_sb", "kz_sb", "qkv_sb", "y12_sb", "relu_sb"))
        edge_exp, prob_exp = signal("edge_exp", 4), signal("prob_exp")
        inc_made = signal("inc_made", 2)
        size_floor, size_inv, deg_rhs_set = signal("size_floor"), signal("size_inv"), signal("deg_rhs_set", 2)
        incw_made = signal("incw_made", 2)
        deg_prep, deg_recip, deg_done = signal("deg_prep", 2), signal("deg_recip"), signal("deg_done", 2)
        hyp1_pre = signal("hyp1_pre", 2)
        r1_based = signal("r1_based", 2)
        scored, max_found, sum_inverted, prob_normed, prob_sb = (
            signal("scored", 2), signal("max_found"), signal("sum_inverted"), signal("prob_normed"), signal("prob_sb"))
        s_sb, s02_sb, e_maxed, y0_sb, rsum_eps, rsum_inv, hop1_sb, hop2_sb = (
            signal("s_sb", 2), signal("s02_sb"), signal("e_maxed"), signal("y0_sb"),
            signal("rsum_eps"), signal("rsum_inv"), signal("hop1_sb", 2), signal("hop2_sb", 2))
        summed = {n: signal(n + "_summed", 1 if n in ("ln0", "ln3") else 2) for n in NORMS if n != "lnh"}
        stated = {n: signal(n + "_stated", 2) for n in NORMS}
        gap_taken = {n: signal(n + "_gap_taken", 2) for n in NORMS}
        gap_used = {n: signal(n + "_gap_used", 2) for n in NORMS}
        averaged = {n: signal(n + "_averaged") for n in NORMS}
        normed = {n: signal(n + "_normed", 2) for n in NORMS}
        rooted = {n: signal(n + "_rooted") for n in NORMS}
        x_b3_made, xx_half, xx_made = (signal(n) for n in ("x_b3_made", "xx_half", "xx_made"))
        alpha_made = signal("alpha_made", 2)
        adj1_kept, adj2_kept, adj3_kept, x3_copied = (
            signal(n, 16) for n in ("adj1_kept", "adj2_kept", "adj3_kept", "x3_copied"))

        def later(pair):
            return not (isinstance(pair, int) and pair == 0)

        def all_steps(eng, step):
            for t in range(LAYERS):
                step(t, range(t + 1))
            with eng.Fori(LAYERS, PAIRS) as t:
                step(t, range(LAYERS))
            for t in range(PAIRS, PAIRS + LAYERS - 1):
                step(t, range(t - PAIRS + 1, LAYERS))

        const_dmas = []

        def const(dst, src):
            const_dmas.append((dst, src))

        for dst, src in ((w1, gcn_w1), (w2, gcn_w2), (w3, gcn_w3), (hyp_w1_nat, hyp_w1), (hyp_w2_nat, hyp_w2),
                         (wv_nat, att_wv), (dif_wv_nat, dif_wv)):
            const(dst[:], src.rearrange("(c p) n -> p c n", p=P))
        const(wqk_nat[:], att_wqk)
        for k in range(HOPS):
            const(w_hop[:, :, k, :], dif_wk[k].rearrange("(c p) n -> p c n", p=P))
            const(bk_rows[:, k, :], dif_bk[k].partition_broadcast(P))
        for g in range(G):
            const(b3_rows[:, g, :], gcn_b3.partition_broadcast(P))
            const(hyp_b2_rows[:, g, :], hyp_b2.partition_broadcast(P))
        const(hyp_b1_rows[:], hyp_b1.partition_broadcast(P))
        const(ab_col[:], dif_ab.partition_broadcast(P))
        for dst, src, n in ((b1_col, gcn_b1, FC), (b2_col, gcn_b2, FC), (gamma_col, hyp_gamma, HC),
                            (beta_col, hyp_beta, HC), (bv_col, dif_bv, FC)):
            for c in range(n):
                const(dst[:, c:c + 1], src[c * P:(c + 1) * P].rearrange("(p a) -> p a", a=1))
        for h in range(2):
            for c in range(FC):
                at = h * F + c * P
                const(aw_cols[:, h, c:c + 1], dif_aw[at:at + P, :])
        CONSTS = 16 * len(const_dmas)

        block = ctx.enter_context(nc.Block())

        @block.sync
        def _(sp):
            for dst, src in const_dmas:
                sp.dma_start(dst, src).then_inc(consts_in, 16)

            def load(t):
                if later(t):
                    sp.wait_ge(adjT_ps.sem, adjT_ps.at(t - 1))
                sp.dma_start(adj_in[:], adj_pairs[t]).then_inc(adj_loaded.sem, 16)
                if later(t):
                    sp.wait_ge(ax_ps.sem, ax_ps.at(t - 1))
                    sp.wait_ge(x_b3_made.sem, x_b3_made.at(t - 1))
                sp.dma_start(x_in[:], x_pairs[t]).then_inc(x_loaded.sem, 16)

            def step(t, on):
                p0, p1, p2, p3 = t, t - 1, t - 2, t - 3
                if 3 in on:
                    if later(p3):
                        sp.wait_ge(normed["ln3"].sem, normed["ln3"].at(p3 - 1))
                        sp.dma_start(out_pairs[p3 - 1], y_out[:]).then_inc(y_stored.sem, 16)
                        sp.wait_ge(summed["ln3"].sem, summed["ln3"].at(p3 - 1))
                    sp.wait_ge(normed["ln2"].sem, normed["ln2"].at(p3))
                    sp.dma_start(x3_kept[:], x3[:]).then_inc(x3_copied.sem, 16)
                if 0 in on and not (isinstance(p0, int) and p0 == PAIRS - 1):
                    load(p0 + 1)
                if 2 in on:
                    sp.wait_ge(ak_ps.sem, ak_ps.at(p2))
                    if 3 in on:
                        sp.wait_ge(alpha_made.sem, alpha_made.at(p3))
                    sp.dma_start(adjT3[:], adjT2[:]).then_inc(adj3_kept.sem, 16)
                if 1 in on:
                    if 2 in on:
                        sp.wait_ge(adj3_kept.sem, adj3_kept.at(p2))
                    sp.wait_ge(adj1_kept.sem, adj1_kept.at(p1))
                    sp.dma_start(adjT2[:], adjT1[:]).then_inc(adj2_kept.sem, 16)
                if 0 in on:
                    sp.wait_ge(gcn_ps.sem, gcn_ps.at(p0))
                    sp.wait_ge(deg_rhs_set.sem, deg_rhs_set.at(p0))
                    if 1 in on:
                        sp.wait_ge(adj2_kept.sem, adj2_kept.at(p1))
                    sp.dma_start(adjT1[:], adjT0[:]).then_inc(adj1_kept.sem, 16)

            load(0)
            for t in range(LAYERS):
                step(t, range(t + 1))
            with sp.Fori(LAYERS, PAIRS - 1) as t:
                step(t, range(LAYERS))
            for t in range(PAIRS - 1, PAIRS + LAYERS - 1):
                step(t, range(max(0, t - PAIRS + 1), LAYERS))
            sp.wait_ge(normed["ln3"].sem, normed["ln3"].at(PAIRS - 1))
            sp.dma_start(out_pairs[PAIRS - 1], y_out[:]).then_inc(y_stored.sem, 16)
            sp.wait_ge(y_stored.sem, y_stored.at(PAIRS - 1))

        @block.tensor
        def _(pe):
            mm, turn = nc.tensor.matmul, nc.tensor.transpose
            everything = bank[0] + bank[1] + bank[2] + bank[3]

            pe.wait_ge(consts_in, CONSTS)
            pe.wait_ge(ident_made, 1)
            for c in range(FC):
                for h in range(HC):
                    turn(everything[c][:, h * P:(h + 1) * P], hyp_w1_nat[:, h, c * P:(c + 1) * P], ident[:])
            for h in range(HC):
                for o in range(FC):
                    at = (h % 2) * F + o * P
                    turn(everything[2 + h // 2][:, at:at + P], hyp_w2_nat[:, o, h * P:(h + 1) * P], ident[:])
            for c in range(FC):
                turn(everything[4 + c][:, 0:QK], wqk_nat[:, c * P:(c + 1) * P], ident[:])
                for o in range(FC):
                    turn(everything[4 + c][:, QK + o * P:QK + (o + 1) * P], wv_nat[:, o, c * P:(c + 1) * P], ident[:])
            for o in range(FC):
                for c in range(FC):
                    last = turn(everything[6][:, o * F + c * P:o * F + (c + 1) * P],
                                dif_wv_nat[:, c, o * P:(o + 1) * P], ident[:])
            last.then_inc(weights_turned, 1)
            pe.wait_ge(weights_kept, 7)
            for h in range(HC):
                mm(everything[7][:, 0:F], beta_col[:, h:h + 1].to_broadcast([P, P]), hyp_w2T[:, h, :],
                   start=(h == 0), stop=(h == HC - 1))
            for c in range(FC):
                for o in range(FC):
                    mm(everything[7][:, F + 2 * c:F + 2 * c + 2], dif_wvT[:, o, c * P:(c + 1) * P], aw_cols[:, :, o],
                       start=(o == 0), stop=(o == FC - 1))
            for o in range(FC):
                last = mm(everything[7][:, F + 8:F + 10], bv_col[:, o:o + 1].to_broadcast([P, P]), aw_cols[:, :, o],
                          start=(o == 0), stop=(o == FC - 1))
            last.then_inc(shifts_made, 1)
            pe.wait_ge(consts_set, 2)
            pe.wait_ge(setup_done, 4)

            def turn_x(dst, src):
                for c in range(FC):
                    for g in range(G):
                        at = (c * G + g) * N
                        last = turn(dst[:, at:at + N], src[:, g, c * P:(c + 1) * P], ident[:])
                return last

            def nodes_mix(dst, src, mix):
                for c in range(FC):
                    for g in range(G):
                        at = (c * G + g) * N
                        last = mm(dst[:, at:at + N], src[:, g, c * P:(c + 1) * P], mix[:, g, :], start=True, stop=True)
                return last

            def weigh(dst, srcT, w):
                for g in range(G):
                    for c in range(FC):
                        last = mm(dst[:, g * F:(g + 1) * F], srcT[:, c, g, :], w[:, c, :],
                                  start=(c == 0), stop=(c == FC - 1))
                return last

            def step(t, on):
                p0, p1, p2, p3 = t, t - 1, t - 2, t - 3
                if 0 in on:
                    pe.wait_ge(adj_loaded.sem, adj_loaded.at(p0))
                    if later(p0):
                        pe.wait_ge(summed["ln0"].sem, summed["ln0"].at(p0 - 1))
                    for g in range(G):
                        last = turn(bank[0][0][:, g * N:(g + 1) * N], adj_in[:, g, :], ident[:])
                    last.then_inc(adjT_ps.sem, 1)
                if 3 in on:
                    pe.wait_ge(normed["ln2"].sem, normed["ln2"].at(p3))
                    if later(p3):
                        pe.wait_ge(hop1_sb.sem, hop1_sb.at(p3 - 1))
                    turn_x(bank[3][0], x3).then_inc(x3T_ps.sem, 1)
                if 1 in on:
                    pe.wait_ge(incw_made.sem, incw_made.at(p1))
                    pe.wait_ge(deg_rhs_set.sem, deg_rhs_set.at(p1))
                    if later(p1):
                        pe.wait_ge(kz_sb.sem, kz_sb.at(p1 - 1, 1))
                    for g in range(G):
                        mm(bank[1][1][:, g * N:(g + 1) * N], incT[:, g, :], incT_w[:, g, :], start=True, stop=True)
                    for g in range(G):
                        last = mm(bank[1][1][:, G * N + 2 * g:G * N + 2 * g + 2], incT[:, g, :], deg_rhs[:, g, :],
                                  start=True, stop=True)
                    last.then_inc(k_ps.sem, 1)
                    pe.wait_ge(k_sb.sem, k_sb.at(p1))
                    pe.wait_ge(normed["ln0"].sem, normed["ln0"].at(p1))
                    if later(p1):
                        pe.wait_ge(summed["ln1"].sem, summed["ln1"].at(p1 - 1))
                    nodes_mix(bank[1][0], x1, kmat).then_inc(kx_ps.sem, 1)
                if 0 in on:
                    pe.wait_ge(adjT_sb.sem, adjT_sb.at(p0))
                    pe.wait_ge(x_loaded.sem, x_loaded.at(p0))
                    if later(p0):
                        pe.wait_ge(s3_sb.sem, s3_sb.at(p0 - 1))
                    nodes_mix(bank[0][1], x_in, adjT0).then_inc(ax_ps.sem, 1)
                if 3 in on:
                    pe.wait_ge(x3T_sb.sem, x3T_sb.at(p3))
                    if later(p3):
                        pe.wait_ge(hop2_sb.sem, hop2_sb.at(p3 - 1))
                    for g in range(G):
                        for c in range(FC):
                            last = mm(bank[3][1][:, 2 * g:2 * g + 2], x3T[:, c, g, :], wa[:, c, :],
                                      start=(c == 0), stop=(c == FC - 1))
                    last.then_inc(s_ps.sem, 1)
                if 1 in on:
                    pe.wait_ge(kx_sb.sem, kx_sb.at(p1))
                    for g in range(G):
                        for c in range(FC):
                            last = mm(bank[1][1 - g][:, 0:DH], kxT[:, c, g, :], hyp_w1T[:, c, :],
                                      start=(c == 0), stop=(c == FC - 1))
                        last.then_inc(hyp1_ps.sem, 1)
                if 2 in on:
                    pe.wait_ge(normed["ln1"].sem, normed["ln1"].at(p2))
                    if later(p2):
                        pe.wait_ge(prob_sb.sem, prob_sb.at(p2 - 1))
                    turn_x(bank[2][0], x2).then_inc(x2T_ps.sem, 1)
                if 0 in on:
                    pe.wait_ge(ax_sb.sem, ax_sb.at(p0))
                    for h in range(FC):
                        for c in range(FC):
                            last = mm(bank[0][0][:, h * G * N:(h + 1) * G * N], w1[:, c, h * P:(h + 1) * P],
                                      axT[:, c, :, :], start=(c == 0), stop=(c == FC - 1))
                    last.then_inc(h1_ps.sem, 1)
                if 3 in on:
                    pe.wait_ge(s_sb.sem, s_sb.at(p3))
                    for g in range(G):
                        last = turn(bank[3][0][:, g * N:(g + 1) * N], s_cols[:, g, 1:2].to_broadcast([P, P]), ident[:])
                    last.then_inc(s_row_ps.sem, 1)
                if 2 in on:
                    pe.wait_ge(x2T_sb.sem, x2T_sb.at(p2))
                    for g in range(G):
                        for c in range(FC):
                            last = mm(bank[2][1 - g][:, 0:QKV], x2T[:, c, g, :], w_qkv[:, c, :],
                                      start=(c == 0), stop=(c == FC - 1))
                        last.then_inc(qkv_ps.sem, 1)
                if 0 in on:
                    pe.wait_ge(h1_sb.sem, h1_sb.at(p0))
                    weigh(bank[0][1], h1T, w2).then_inc(s2_ps.sem, 1)
                if 3 in on:
                    weigh(bank[3][1], x3T, w_hop[:, :, 1, :]).then_inc(y12_ps.sem, 1)
                    pe.wait_ge(edge_exp.sem, edge_exp.at(p3))
                    weigh(bank[3][0], x3T, w_hop[:, :, 2, :]).then_inc(y12_ps.sem, 1)
                if 2 in on:
                    pe.wait_ge(qkv_sb.sem, qkv_sb.at(p2))
                    pe.wait_ge(adj2_kept.sem, adj2_kept.at(p2))
                    for g in range(G):
                        last = mm(bank[2][1][:, g * DA:(g + 1) * DA], adjT2[:, g, :], qkv[:, g, DA:2 * DA],
                                  start=True, stop=True)
                    last.then_inc(ak_ps.sem, 1)
                if 0 in on:
                    pe.wait_ge(s2_sb.sem, s2_sb.at(p0))
                    nodes_mix(bank[0][0], s2, adjT0).then_inc(as2_ps.sem, 1)
                if 1 in on:
                    for g in range(G):
                        pe.wait_ge(normed["lnh"].sem, normed["lnh"].at(p1, g + 1))
                        for h in range(HC):
                            last = mm(bank[1][1 - g][:, h * N:(h + 1) * N], z[:, g, h * P:(h + 1) * P], kmat[:, g, :],
                                      start=True, stop=True)
                        last.then_inc(kz_ps.sem, 1)
                if 2 in on:
                    pe.wait_ge(scored.sem, scored.at(p2))
                    mm(bank[2][0][0:G, 0:N], score[:], ident[:], start=True, stop=True).then_inc(score_ps.sem, 1)
                if 0 in on:
                    pe.wait_ge(h2_sb.sem, h2_sb.at(p0))
                    weigh(bank[0][1], h2T, w3).then_inc(s3_ps.sem, 1)
                if 3 in on:
                    pe.wait_ge(y12_sb.sem, y12_sb.at(p3, 1))
                    weigh(bank[3][1], x3T, w_hop[:, :, 0, :]).then_inc(y0_ps.sem, 1)
                    pe.wait_ge(y12_sb.sem, y12_sb.at(p3))
                    pe.wait_ge(alpha_made.sem, alpha_made.at(p3))
                    for g in range(G):
                        last = mm(bank[3][0][:, g:g + 1], alphaT[:, g, :], ones[:], start=True, stop=True)
                    last.then_inc(sum_ps.sem, 1)
                if 2 in on:
                    pe.wait_ge(prob_normed.sem, prob_normed.at(p2))
                    mm(bank[2][0][:, 0:G], prob_row[:], ident[0:G, 0:G], start=True, stop=True).then_inc(prob_ps.sem, 1)
                if 0 in on:
                    pe.wait_ge(s3_sb.sem, s3_sb.at(p0))
                    for g in range(G):
                        last = mm(bank[0][0][:, g * F:(g + 1) * F], adjT0[:, g, :], s3[:, g, :], start=True, stop=True)
                    last.then_inc(gcn_ps.sem, 1)
                if 3 in on:
                    pe.wait_ge(rsum_eps.sem, rsum_eps.at(p3))
                    for g in range(G):
                        last = mm(bank[3][0][:, g * F:(g + 1) * F], alphaT[:, g, :], y2[:, g, :], start=True, stop=True)
                    last.then_inc(hop1_ps.sem, 1)
                if 1 in on:
                    pe.wait_ge(kz_sb.sem, kz_sb.at(p1))
                    for g in range(G):
                        for h in range(HC):
                            last = mm(bank[1][0][:, g * F:(g + 1) * F], kzT[:, g, h, :], hyp_w2g[:, h, :],
                                      start=(h == 0), stop=(h == HC - 1))
                    last.then_inc(hyp2_ps.sem, 1)
                if 3 in on:
                    pe.wait_ge(hop1_sb.sem, hop1_sb.at(p3))
                    pe.wait_ge(y0_sb.sem, y0_sb.at(p3))
                    for g in range(G):
                        last = mm(bank[3][1][:, g * F:(g + 1) * F], alphaT[:, g, :], hop1[:, g, :],
                                  start=True, stop=True)
                    last.then_inc(hop2_ps.sem, 1)

            all_steps(pe, step)

        @block.scalar
        def _(act):
            def copy(dst, src):
                return nc.scalar.activation(dst, src, ACT.Copy)

            def flat(a):
                return a[:].rearrange("p a b c -> p (a b c)") if len(a.shape) == 4 else a[:].rearrange("p a b -> p (a b)")

            def step(t, on):
                p0, p1, p2, p3 = t, t - 1, t - 2, t - 3
                if 0 in on:
                    act.wait_ge(adjT_ps.sem, adjT_ps.at(p0))
                    if later(p0):
                        act.wait_ge(adj1_kept.sem, adj1_kept.at(p0 - 1))
                    copy(flat(adjT0), bank[0][0][:, 0:G * N]).then_inc(adjT_sb.sem, 1)
                if 3 in on:
                    act.wait_ge(x3T_ps.sem, x3T_ps.at(p3))
                    copy(flat(x3T), bank[3][0][:]).then_inc(x3T_sb.sem, 1)
                if 1 in on:
                    act.wait_ge(k_ps.sem, k_ps.at(p1))
                    if later(p1):
                        act.wait_ge(deg_done.sem, deg_done.at(p1 - 1))
                    copy(kdeg[:], bank[1][1][:, 0:G * N + 2 * G]).then_inc(k_sb.sem, 1)
                    act.wait_ge(kx_ps.sem, kx_ps.at(p1))
                    copy(flat(kxT), bank[1][0][:]).then_inc(kx_sb.sem, 1)
                if 0 in on:
                    act.wait_ge(ax_ps.sem, ax_ps.at(p0))
                    copy(flat(axT), bank[0][1][:]).then_inc(ax_sb.sem, 1)
                if 1 in on:
                    for g in range(G):
                        act.wait_ge(hyp1_pre.sem, hyp1_pre.at(p1, g + 1))
                        if later(p1):
                            act.wait_ge(normed["lnh"].sem, normed["lnh"].at(p1 - 1, g + 1))
                        nc.scalar.activation(h_act[:, g, :], h_pre[:, g, :], ACT.Relu).then_inc(relu_sb.sem, 1)
                if 2 in on:
                    act.wait_ge(x2T_ps.sem, x2T_ps.at(p2))
                    copy(flat(x2T), bank[2][0][:]).then_inc(x2T_sb.sem, 1)
                if 0 in on:
                    act.wait_ge(h1_ps.sem, h1_ps.at(p0))
                    for c in range(FC):
                        nc.scalar.activation(h1T[:, c, :, :], bank[0][0][:, c * G * N:(c + 1) * G * N], ACT.Relu,
                                             bias=b1_col[:, c:c + 1]).then_inc(h1_sb.sem, 1)
                if 3 in on:
                    act.wait_ge(s_row_ps.sem, s_row_ps.at(p3))
                    act.wait_ge(s02_sb.sem, s02_sb.at(p3))
                    if later(p3):
                        act.wait_ge(e_maxed.sem, e_maxed.at(p3 - 1))
                    for g in range(G):
                        row = bank[3][0][:, g * N:(g + 1) * N]
                        nc.scalar.activation(e_pos[:, g, :], row, ACT.Exp,
                                             bias=s_cols[:, g, 0:1]).then_inc(edge_exp.sem, 1)
                        nc.scalar.activation(e_neg[:, g, :], row, ACT.Exp, scale=0.2,
                                             bias=s_col02[:, g:g + 1]).then_inc(edge_exp.sem, 1)
                if 2 in on:
                    for g in range(G):
                        act.wait_ge(qkv_ps.sem, qkv_ps.at(p2, g + 1))
                        if later(p2):
                            act.wait_ge(summed["ln2"].sem, summed["ln2"].at(p2 - 1))
                        copy(qkv[:, g, :], bank[2][1 - g][:, 0:QKV]).then_inc(qkv_sb.sem, 1)
                if 0 in on:
                    act.wait_ge(s2_ps.sem, s2_ps.at(p0))
                    copy(flat(s2), bank[0][1][:]).then_inc(s2_sb.sem, 1)
                if 3 in on:
                    act.wait_ge(y12_ps.sem, y12_ps.at(p3, 1))
                    if later(p3):
                        act.wait_ge(hop1_sb.sem, hop1_sb.at(p3 - 1))
                    copy(flat(y1), bank[3][1][:]).then_inc(y12_sb.sem, 1)
                    act.wait_ge(y12_ps.sem, y12_ps.at(p3, 2))
                    copy(flat(y2), bank[3][0][:]).then_inc(y12_sb.sem, 1)
                if 0 in on:
                    act.wait_ge(as2_ps.sem, as2_ps.at(p0))
                    for c in range(FC):
                        nc.scalar.activation(h2T[:, c, :, :], bank[0][0][:, c * G * N:(c + 1) * G * N], ACT.Relu,
                                             bias=b2_col[:, c:c + 1]).then_inc(h2_sb.sem, 1)
                if 1 in on:
                    for g in range(G):
                        act.wait_ge(kz_ps.sem, kz_ps.at(p1, g + 1))
                        copy(kzT[:, g, :, :].rearrange("p h n -> p (h n)"),
                             bank[1][1 - g][:]).then_inc(kz_sb.sem, 1)
                if 2 in on:
                    act.wait_ge(max_found.sem, max_found.at(p2))
                    if later(p2):
                        act.wait_ge(prob_normed.sem, prob_normed.at(p2 - 1))
                    nc.scalar.activation(prob_e[:], bank[2][0][0:G, 0:N], ACT.Exp, bias=neg_max[:],
                                         accum_out=prob_sum[:]).then_inc(prob_exp.sem, 1)
                if 0 in on:
                    act.wait_ge(s3_ps.sem, s3_ps.at(p0))
                    copy(flat(s3), bank[0][1][:]).then_inc(s3_sb.sem, 1)

            act.wait_ge(consts_in, CONSTS)
            all_steps(act, step)

        @block.vector
        def _(dve):
            v = nc.vector
            everything = bank[0] + bank[1] + bank[2] + bank[3]

            dve.wait_ge(weights_turned, 1)
            for c in range(FC):
                v.tensor_copy(hyp_w1T[:, c, :], everything[c][:]).then_inc(weights_kept, 1)
            for b in range(2):
                v.tensor_copy(hyp_w2T[:, 2 * b:2 * b + 2, :].rearrange("p a b -> p (a b)"),
                              everything[2 + b][:]).then_inc(weights_kept, 1)
            for c in range(FC):
                v.tensor_copy(w_qkv[:, c, :], everything[4 + c][:, 0:QKV]).then_inc(weights_kept, 1)
            v.tensor_copy(dif_wvT[:].rearrange("p a b -> p (a b)"), everything[6][:]).then_inc(weights_kept, 1)
            dve.wait_ge(weights_kept, 7)
            dve.wait_ge(consts_in, CONSTS)
            for h in range(HC):
                v.tensor_scalar(hyp_w2g[:, h, :], hyp_w2T[:, h, :], gamma_col[:, h:h + 1], None, ALU.mult)
            v.tensor_tensor(bk_tmp[:], bk_rows[:, 0, :], bk_rows[:, 1, :], ALU.add).then_inc(bias_summed, 1)
            dve.wait_ge(bias_summed, 1)
            for g in range(G):
                v.tensor_tensor(bk_sum[:, g, :], bk_tmp[:], bk_rows[:, 2, :], ALU.add)
            dve.wait_ge(shifts_made, 1)
            v.tensor_copy(hyp_shift[:], everything[7][:, 0:F])
            v.tensor_copy(wa[:].rearrange("p a b -> p (a b)"), everything[7][:, F:F + 2 * FC]).then_inc(setup_done, 1)
            v.tensor_copy(s_part[:], everything[7][:, F + 8:F + 10]).then_inc(setup_done, 1)
            dve.wait_ge(setup_done, 2)
            v.tensor_tensor(s_const[:], s_part[:, 0:1], s_part[:, 1:2], ALU.add).then_inc(setup_done, 1)
            dve.wait_ge(setup_done, 3)
            v.tensor_tensor(s_const[:], s_const[:], ab_col[:], ALU.add).then_inc(setup_done, 1)
            dve.wait_ge(setup_done, 4)
            dve.wait_ge(consts_set, 2)

            def flat(a):
                return a[:].rearrange("p a b -> p (a b)")

            def statistics(n, p, src, ready):
                for g in range(G):
                    ready(g)
                    v.bn_stats(stats[n][:, g, :], src[:, g, :]).then_inc(stated[n].sem, 1)
                half_mean = stats[n][:, :, 1::3]
                half_sum = stats[n][:, :, 2::3]
                size = src.shape[2]
                dve.wait_ge(stated[n].sem, stated[n].at(p))
                v.tensor_tensor(mean_gap[n][:], half_mean[:, :, 0], half_mean[:, :, 1], ALU.subtract)\
                    .then_inc(gap_taken[n].sem, 1)
                v.scalar_tensor_tensor(square_sum[n][:], half_sum[:, :, 0], EPS * size, half_sum[:, :, 1],
                                       ALU.add, ALU.add).then_inc(gap_taken[n].sem, 1)
                dve.wait_ge(gap_taken[n].sem, gap_taken[n].at(p, 1))
                v.scalar_tensor_tensor(mean[n][:], mean_gap[n][:], -0.5, half_mean[:, :, 0],
                                       ALU.mult, ALU.add).then_inc(gap_used[n].sem, 1)
                v.scalar_tensor_tensor(gap_square[n][:], mean_gap[n][:], 0.25, mean_gap[n][:],
                                       ALU.mult, ALU.mult).then_inc(gap_used[n].sem, 1)
                dve.wait_ge(gap_used[n].sem, gap_used[n].at(p))
                v.scalar_tensor_tensor(var_eps[n][:], square_sum[n][:], 1.0 / size, gap_square[n][:],
                                       ALU.mult, ALU.add).then_inc(averaged[n].sem, 1)

            def normalise(n, p, dst, src):
                dve.wait_ge(rooted[n].sem, rooted[n].at(p))
                for g in range(G):
                    v.tensor_scalar(dst[:, g, :], src[:, g, :], mean[n][:, g:g + 1], rstd[n][:, g:g + 1],
                                    ALU.subtract, ALU.mult).then_inc(normed[n].sem, 1)

            def step(t, on):
                p0, p1, p2, p3 = t, t - 1, t - 2, t - 3
                if 1 in on:
                    dve.wait_ge(k_sb.sem, k_sb.at(p1))
                    v.tensor_scalar(deg_pos[:], deg[:, :, 1], 0.0, None, ALU.is_gt).then_inc(deg_prep.sem, 1)
                    v.tensor_scalar(deg_safe[:], deg[:, :, 1], TINY, None, ALU.max).then_inc(deg_prep.sem, 1)
                    dve.wait_ge(deg_prep.sem, deg_prep.at(p1))
                    v.reciprocal(deg_rec[:], deg_safe[:]).then_inc(deg_recip.sem, 1)
                    dve.wait_ge(deg_recip.sem, deg_recip.at(p1))
                    v.tensor_tensor(deg_inv[:], deg_rec[:], deg_pos[:], ALU.mult).then_inc(deg_done.sem, 1)
                    dve.wait_ge(deg_done.sem, deg_done.at(p1, 1))
                    v.tensor_tensor(row_sum[:], deg_inv[:], deg[:, :, 0], ALU.mult).then_inc(deg_done.sem, 1)
                if 3 in on:
                    dve.wait_ge(s_ps.sem, s_ps.at(p3))
                    s_view = bank[3][1][:, 0:2 * G].rearrange("p (g j) -> p g j", j=2)
                    v.tensor_scalar(s_cols[:, :, 0], s_view[:, :, 0], s_const[:], None, ALU.add).then_inc(s_sb.sem, 1)
                    v.tensor_copy(s_cols[:, :, 1], s_view[:, :, 1]).then_inc(s_sb.sem, 1)
                    dve.wait_ge(s_sb.sem, s_sb.at(p3, 1))
                    v.tensor_scalar(s_col02[:], s_cols[:, :, 0], 0.2, None, ALU.mult).then_inc(s02_sb.sem, 1)
                if 0 in on:
                    dve.wait_ge(adjT_sb.sem, adjT_sb.at(p0))
                    for g in range(G):
                        v.tensor_scalar(incT[:, g, :], adjT0[:, g, :], 0.0, None, ALU.not_equal, ALU.add,
                                        accum_out=edge_size[:, g:g + 1]).then_inc(inc_made.sem, 1)
                if 1 in on:
                    for g in range(G):
                        dve.wait_ge(hyp1_ps.sem, hyp1_ps.at(p1, g + 1))
                        dve.wait_ge(deg_done.sem, deg_done.at(p1))
                        v.scalar_tensor_tensor(h_pre[:, g, :], bank[1][1 - g][:, 0:DH], deg_inv[:, g:g + 1],
                                               hyp_b1_rows[:], ALU.mult, ALU.add).then_inc(hyp1_pre.sem, 1)
                if 0 in on:
                    dve.wait_ge(inc_made.sem, inc_made.at(p0))
                    v.tensor_scalar(edge_size1[:], edge_size[:], 1.0, None, ALU.max).then_inc(size_floor.sem, 1)
                    dve.wait_ge(size_floor.sem, size_floor.at(p0))
                    v.reciprocal(edge_inv[:], edge_size1[:]).then_inc(size_inv.sem, 1)
                    dve.wait_ge(size_inv.sem, size_inv.at(p0))
                    v.tensor_tensor(deg_rhs[:, :, 0], edge_inv[:], edge_size[:], ALU.mult).then_inc(deg_rhs_set.sem, 1)
                    v.tensor_copy(deg_rhs[:, :, 1], adjT0[:, :, 0]).then_inc(deg_rhs_set.sem, 1)
                    for g in range(G):
                        v.tensor_scalar(incT_w[:, g, :], incT[:, g, :], edge_inv[:, g:g + 1], None,
                                        ALU.mult).then_inc(incw_made.sem, 1)
                if 1 in on:
                    statistics("lnh", p1, h_act, lambda g: dve.wait_ge(relu_sb.sem, relu_sb.at(p1, g + 1)))
                if 3 in on:
                    dve.wait_ge(edge_exp.sem, edge_exp.at(p3))
                    if later(p3):
                        dve.wait_ge(alpha_made.sem, alpha_made.at(p3 - 1))
                    v.tensor_tensor(flat(e_max), flat(e_pos), flat(e_neg), ALU.max).then_inc(e_maxed.sem, 1)
                if 1 in on:
                    normalise("lnh", p1, z, h_act)
                if 1 in on:
                    dve.wait_ge(xx_made.sem, xx_made.at(p1))
                    for g in range(G):
                        v.scalar_tensor_tensor(r1_base[:, g, :], hyp_shift[:], row_sum[:, g:g + 1], xx[:, g, :],
                                               ALU.mult, ALU.add).then_inc(r1_based.sem, 1)
                if 2 in on:
                    dve.wait_ge(ak_ps.sem, ak_ps.at(p2))
                    for g in range(G):
                        v.scalar_tensor_tensor(qak[:, g, :], bank[2][1][:, g * DA:(g + 1) * DA], INV_SCALE,
                                               qkv[:, g, 0:DA], ALU.mult, ALU.mult,
                                               accum_out=score[:, g:g + 1]).then_inc(scored.sem, 1)
                    dve.wait_ge(score_ps.sem, score_ps.at(p2))
                    v.tensor_reduce(neg_max[:], bank[2][0][0:G, 0:N], AX.X, ALU.max, negate=True).then_inc(max_found.sem, 1)
                if 3 in on:
                    dve.wait_ge(y0_ps.sem, y0_ps.at(p3))
                    v.tensor_tensor(flat(y0), bank[3][1][:], flat(bk_sum), ALU.add).then_inc(y0_sb.sem, 1)
                if 2 in on:
                    dve.wait_ge(prob_exp.sem, prob_exp.at(p2))
                    v.reciprocal(prob_inv[:], prob_sum[:]).then_inc(sum_inverted.sem, 1)
                    dve.wait_ge(sum_inverted.sem, sum_inverted.at(p2))
                    v.tensor_scalar(prob_row[:], prob_e[:], prob_inv[:], None, ALU.mult).then_inc(prob_normed.sem, 1)
                if 3 in on:
                    dve.wait_ge(sum_ps.sem, sum_ps.at(p3))
                    v.tensor_scalar(sum_eps[:], bank[3][0][:, 0:G], 1e-12, None, ALU.add).then_inc(rsum_eps.sem, 1)
                    dve.wait_ge(rsum_eps.sem, rsum_eps.at(p3))
                    v.reciprocal(sum_inv[:], sum_eps[:]).then_inc(rsum_inv.sem, 1)
                if 2 in on:
                    dve.wait_ge(prob_ps.sem, prob_ps.at(p2))
                    v.tensor_copy(prob[:], bank[2][0][:, 0:G]).then_inc(prob_sb.sem, 1)
                    dve.wait_ge(prob_sb.sem, prob_sb.at(p2))
                    for g in range(G):
                        v.scalar_tensor_tensor(r2[:, g, :], qkv[:, g, QK:QKV], prob[:, g:g + 1], x2[:, g, :],
                                               ALU.mult, ALU.add).then_inc(summed["ln2"].sem, 1)
                    statistics("ln2", p2, r2, lambda g: dve.wait_ge(summed["ln2"].sem, summed["ln2"].at(p2, g + 1)))
                if 0 in on:
                    dve.wait_ge(gcn_ps.sem, gcn_ps.at(p0))
                    dve.wait_ge(x_b3_made.sem, x_b3_made.at(p0))
                    v.tensor_tensor(flat(r0), bank[0][0][:], flat(x_b3), ALU.add).then_inc(summed["ln0"].sem, 1)
                    statistics("ln0", p0, r0, lambda g: dve.wait_ge(summed["ln0"].sem, summed["ln0"].at(p0)))
                if 3 in on:
                    dve.wait_ge(hop1_ps.sem, hop1_ps.at(p3))
                    dve.wait_ge(rsum_inv.sem, rsum_inv.at(p3))
                    for g in range(G):
                        v.scalar_tensor_tensor(hop1[:, g, :], bank[3][0][:, g * F:(g + 1) * F], sum_inv[:, g:g + 1],
                                               y1[:, g, :], ALU.mult, ALU.add).then_inc(hop1_sb.sem, 1)
                if 2 in on:
                    if 3 in on:
                        dve.wait_ge(x3_copied.sem, x3_copied.at(p3))
                    normalise("ln2", p2, x3, r2)
                if 0 in on:
                    if later(p0):
                        dve.wait_ge(xx_made.sem, xx_made.at(p0 - 1))
                    normalise("ln0", p0, x1, r0)
                if 1 in on:
                    dve.wait_ge(hyp2_ps.sem, hyp2_ps.at(p1))
                    dve.wait_ge(r1_based.sem, r1_based.at(p1))
                    for g in range(G):
                        v.scalar_tensor_tensor(r1[:, g, :], bank[1][0][:, g * F:(g + 1) * F], deg_inv[:, g:g + 1],
                                               r1_base[:, g, :], ALU.mult, ALU.add).then_inc(summed["ln1"].sem, 1)
                    statistics("ln1", p1, r1, lambda g: dve.wait_ge(summed["ln1"].sem, summed["ln1"].at(p1, g + 1)))
                if 3 in on:
                    dve.wait_ge(hop2_ps.sem, hop2_ps.at(p3))
                    for g in range(G):
                        v.scalar_tensor_tensor(hop2[:, g, :], bank[3][1][:, g * F:(g + 1) * F], sum_inv[:, g:g + 1],
                                               y0[:, g, :], ALU.mult, ALU.add).then_inc(hop2_sb.sem, 1)
                if 1 in on:
                    normalise("ln1", p1, x2, r1)
                if 3 in on:
                    dve.wait_ge(hop2_sb.sem, hop2_sb.at(p3))
                    dve.wait_ge(x3_copied.sem, x3_copied.at(p3))
                    v.scalar_tensor_tensor(flat(r3), flat(hop2), 0.0, flat(x3_kept), ALU.max, ALU.add)\
                        .then_inc(summed["ln3"].sem, 1)
                    statistics("ln3", p3, r3, lambda g: dve.wait_ge(summed["ln3"].sem, summed["ln3"].at(p3)))
                    if later(p3):
                        dve.wait_ge(y_stored.sem, y_stored.at(p3 - 1))
                    normalise("ln3", p3, y_out, r3)

            all_steps(dve, step)

        @block.gpsimd
        def _(pool):
            gp = nc.gpsimd
            gp.memset(ident[:], 0.0).then_inc(ident_zero, 1)
            pool.wait_ge(ident_zero, 1)
            gp.affine_select(out=ident[:], in_=ident[:], compare_op=ALU.not_equal, fill=1.0, base=0,
                             pattern=[[-1, P]], channel_multiplier=1).then_inc(ident_made, 1)
            gp.memset(ones[:], 1.0).then_inc(consts_set, 1)
            gp.memset(neg_half[:], -0.5).then_inc(consts_set, 1)
            pool.wait_ge(consts_set, 2)
            pool.wait_ge(consts_in, CONSTS)

            def flat(a):
                return a[:].rearrange("p a b -> p (a b)")

            def root(n, p):
                pool.wait_ge(averaged[n].sem, averaged[n].at(p))
                if later(p):
                    pool.wait_ge(normed[n].sem, normed[n].at(p - 1))
                gp.tensor_tensor(rstd[n][:], var_eps[n][:], neg_half[:], ALU.pow).then_inc(rooted[n].sem, 1)

            def step(t, on):
                p0, p1, p2, p3 = t, t - 1, t - 2, t - 3
                if 1 in on:
                    pool.wait_ge(normed["ln0"].sem, normed["ln0"].at(p1))
                    if later(p1):
                        pool.wait_ge(r1_based.sem, r1_based.at(p1 - 1))
                    gp.tensor_tensor(flat(xx), flat(x1), flat(hyp_b2_rows), ALU.add).then_inc(xx_half.sem, 1)
                    pool.wait_ge(xx_half.sem, xx_half.at(p1))
                    gp.tensor_tensor(flat(xx), flat(xx), flat(x1), ALU.add).then_inc(xx_made.sem, 1)
                if 0 in on:
                    pool.wait_ge(x_loaded.sem, x_loaded.at(p0))
                    if later(p0):
                        pool.wait_ge(summed["ln0"].sem, summed["ln0"].at(p0 - 1))
                    gp.tensor_tensor(flat(x_b3), flat(x_in), flat(b3_rows), ALU.add).then_inc(x_b3_made.sem, 1)
                if 1 in on:
                    root("lnh", p1)
                if 3 in on:
                    pool.wait_ge(e_maxed.sem, e_maxed.at(p3))
                    pool.wait_ge(adj3_kept.sem, adj3_kept.at(p3))
                    if later(p3):
                        pool.wait_ge(hop2_ps.sem, hop2_ps.at(p3 - 1))
                    for g in range(G):
                        gp.tensor_tensor(alphaT[:, g, :], e_max[:, g, :], adjT3[:, g, :],
                                         ALU.mult).then_inc(alpha_made.sem, 1)
                if 2 in on:
                    root("ln2", p2)
                if 0 in on:
                    root("ln0", p0)
                if 1 in on:
                    root("ln1", p1)
                if 3 in on:
                    root("ln3", p3)

            all_steps(pool, step)

    return nc


_INS = ["x", "adj", "L0_gnn_W1", "L0_gnn_b1", "L0_gnn_W2", "L0_gnn_b2", "L0_gnn_W3", "L0_gnn_b3",
        "L1_gnn_W1", "L1_gnn_b1", "L1_gnn_gamma", "L1_gnn_beta", "L1_gnn_W2", "L1_gnn_b2",
        "L2_gnn_W_qk", "L2_gnn_W_v",
        "L3_gnn_Wv", "L3_gnn_bv", "L3_gnn_aw", "L3_gnn_ab", "L3_gnn_Wk", "L3_gnn_bk"]


def kernel(**inputs):
    import numpy as np
    import concourse.bacc as bacc
    from concourse.bass_utils import run_bass_kernel_spmd

    nc = bacc.Bacc("TRN2", target_bir_lowering=False, num_devices=1)
    arrays, args = {}, []
    for name in _INS:
        a = np.ascontiguousarray(inputs[name])
        arrays[f"in_{name}"] = a
        args.append(nc.dram_tensor(f"in_{name}", a.shape, mybir.dt.from_np(a.dtype), kind="ExternalInput").ap())
    args.append(nc.dram_tensor("out", inputs["x"].shape, F32, kind="ExternalOutput").ap())
    graph_block_kernel(nc, *args)
    return run_bass_kernel_spmd(nc, [arrays], core_ids=[0]).results[0]["out"]
```

```python
from contextlib import ExitStack

import concourse.bass as bass
from concourse import mybir

ALU = mybir.AluOpType
ACT = mybir.ActivationFunctionType
AX = mybir.AxisListType
F32 = mybir.dt.float32
F32R = mybir.dt.float32r

P = 128
EPS = 1e-5
TINY = 1.1754944e-38


class Signal:

    def __init__(self, sem, per_pair):
        self.sem, self.per = sem, per_pair

    def at(self, pair, k=None):
        return pair * self.per + (self.per if k is None else k)


def graph_block_kernel(
    nc, x, adj,
    gcn_w1, gcn_b1, gcn_w2, gcn_b2, gcn_w3, gcn_b3,
    hyp_w1, hyp_b1, hyp_gamma, hyp_beta, hyp_w2, hyp_b2,
    att_wqk, att_wv,
    dif_wv, dif_bv, dif_aw, dif_ab, dif_wk, dif_bk,
    out,
):
    B, N, F = x.shape
    G = 2
    PAIRS = B // G
    FC = F // P
    DH = hyp_w1.shape[0]
    HC = DH // P
    QK = att_wqk.shape[0]
    DA = QK // 2
    QKV = QK + F
    HOPS = dif_wk.shape[0]
    INV_SCALE = 1.0 / DA ** 0.5
    assert N == P and F == 2 * P and HC == 4 and HOPS == 3
    LAYERS = 4
    STAGES = LAYERS + 1

    x_pairs = x.rearrange("(s g) n f -> s n g f", g=G)
    adj_pairs = adj.rearrange("(s g) n m -> s n g m", g=G)
    out_pairs = out.rearrange("(s g) n f -> s n g f", g=G)

    with ExitStack() as ctx:
        def sb(name, shape, dtype=F32):
            return ctx.enter_context(nc.sbuf_tensor(name, shape, dtype))

        def halves(name, shape):
            return sb(name + "_hi", shape, F32R), sb(name + "_lo", shape, F32R)

        def sem(name):
            return ctx.enter_context(nc.semaphore(name))

        def signal(name, per_pair=1):
            return Signal(sem(name), per_pair)

        ident = sb("ident", [P, P])
        ones = sb("ones", [P, 1])
        neg_half = sb("neg_half", [P, G])
        w1_raw = sb("w1_raw", [P, FC, F])
        w1 = halves("w1", [P, FC, F])
        w2 = sb("w2", [P, FC, F])
        w3 = sb("w3", [P, FC, F])
        b1_col = sb("b1_col", [P, FC])
        b2_col = sb("b2_col", [P, FC])
        b3_rows = sb("b3_rows", [P, G, F])
        hyp_w1_nat = sb("hyp_w1_nat", [P, HC, F])
        hyp_w1T = halves("hyp_w1T", [P, FC, DH])
        hyp_b1_rows = sb("hyp_b1_rows", [P, DH])
        gamma_col = sb("gamma_col", [P, HC])
        beta_col = sb("beta_col", [P, HC])
        hyp_w2_nat = sb("hyp_w2_nat", [P, FC, DH])
        hyp_w2T = sb("hyp_w2T", [P, HC, F])
        hyp_w2g_raw = sb("hyp_w2g_raw", [P, HC, F])
        hyp_w2g = halves("hyp_w2g", [P, HC, F])
        hyp_shift = sb("hyp_shift", [P, F])
        hyp_b2_rows = sb("hyp_b2_rows", [P, G, F])
        wqk_nat = sb("wqk_nat", [P, F])
        wv_nat = sb("wv_nat", [P, FC, F])
        w_qkv = halves("w_qkv", [P, FC, QKV])
        dif_wv_nat = sb("dif_wv_nat", [P, FC, F])
        dif_wvT = sb("dif_wvT", [P, FC, F])
        bv_col = sb("bv_col", [P, FC])
        aw_cols = sb("aw_cols", [P, 2, FC])
        ab_col = sb("ab_col", [P, 1])
        wa_raw = sb("wa_raw", [P, FC, 2])
        wa = halves("wa", [P, FC, 2])
        s_const = sb("s_const", [P, 1])
        s_part = sb("s_part", [P, 2])
        w_hop_raw = sb("w_hop_raw", [P, FC, HOPS, F])
        w_hop = halves("w_hop", [P, FC, HOPS, F])
        bk_rows = sb("bk_rows", [P, HOPS, F])
        bk_tmp = sb("bk_tmp", [P, F])
        bk_sum = sb("bk_sum", [P, G, F])

        x_in = sb("x_in", [P, G, F])
        adj_in = sb("adj_in", [P, G, N])
        adjT0 = sb("adjT0", [P, G, N])
        x_b3 = sb("x_b3", [P, G, F])
        axT = halves("axT", [P, FC, G, N])
        h1T = sb("h1T", [P, FC, G, N])
        s2 = sb("s2", [P, G, F])
        h2T = sb("h2T", [P, FC, G, N])
        s3 = sb("s3", [P, G, F])
        r0 = sb("r0", [P, G, F])
        x1 = sb("x1", [P, G, F])
        incT = sb("incT", [P, G, N])
        incT_w = sb("incT_w", [P, G, N])
        edge_size = sb("edge_size", [P, G])
        edge_size1 = sb("edge_size1", [P, G])
        edge_inv = sb("edge_inv", [P, G])
        deg_rhs = sb("deg_rhs", [P, G, 2])
        adjT1 = sb("adjT1", [P, G, N])
        kdeg = sb("kdeg", [P, G * N + G * 2])
        kmat = kdeg[:, 0:G * N].rearrange("p (g n) -> p g n", g=G)
        deg = kdeg[:, G * N:G * N + G * 2].rearrange("p (g j) -> p g j", g=G)
        deg_pos = sb("deg_pos", [P, G])
        deg_safe = sb("deg_safe", [P, G])
        deg_rec = sb("deg_rec", [P, G])
        deg_inv = sb("deg_inv", [P, G])
        row_sum = sb("row_sum", [P, G])
        kxT = halves("kxT", [P, FC, G, N])
        h_pre = sb("h_pre", [P, G, DH])
        h_act = sb("h_act", [P, G, DH])
        z = sb("z", [P, G, DH])
        kzT = halves("kzT", [P, G, HC, N])
        xx = sb("xx", [P, G, F])
        r1_base = sb("r1_base", [P, G, F])
        r1 = sb("r1", [P, G, F])
        x2 = sb("x2", [P, G, F])
        adjT2 = sb("adjT2", [P, G, N])
        x2T = halves("x2T", [P, FC, G, N])
        qkv = sb("qkv", [P, G, QKV])
        qak = sb("qak", [P, G, DA])
        score = sb("score", [P, G])
        neg_max = sb("neg_max", [G, 1])
        prob_e = sb("prob_e", [G, N])
        prob_sum = sb("prob_sum", [G, 1])
        prob_inv = sb("prob_inv", [G, 1])
        prob_row = sb("prob_row", [G, N])
        prob = sb("prob", [P, G])
        r2 = sb("r2", [P, G, F])
        x3 = sb("x3", [P, G, F])
        adjT3 = sb("adjT3", [P, G, N])
        x3T = halves("x3T", [P, FC, G, N])
        s_cols = sb("s_cols", [P, G, 2])
        s_col02 = sb("s_col02", [P, G])
        e_pos = sb("e_pos", [P, G, N])
        e_neg = sb("e_neg", [P, G, N])
        e_max = sb("e_max", [P, G, N])
        alphaT = sb("alphaT", [P, G, N])
        sum_eps = sb("sum_eps", [P, G])
        sum_inv = sb("sum_inv", [P, G])
        y0_plain = sb("y0_plain", [P, G, F])
        y0 = sb("y0", [P, G, F])
        y1 = sb("y1", [P, G, F])
        y2 = sb("y2", [P, G, F])
        hop1 = sb("hop1", [P, G, F])
        hop2 = sb("hop2", [P, G, F])
        x3_kept = sb("x3_kept", [P, G, F])
        r3 = sb("r3", [P, G, F])
        y_out = sb("y_out", [P, G, F])

        NORMS = ("ln0", "lnh", "ln1", "ln2", "ln3")
        stats = {n: sb(n + "_stats", [P, G, 6]) for n in NORMS}
        mean_gap = {n: sb(n + "_mean_gap", [P, G]) for n in NORMS}
        gap_square = {n: sb(n + "_gap_square", [P, G]) for n in NORMS}
        square_sum = {n: sb(n + "_square_sum", [P, G]) for n in NORMS}
        neg_mean = {n: sb(n + "_neg_mean", [P, G]) for n in NORMS}
        shift = {n: sb(n + "_shift", [P, G]) for n in NORMS}
        var_eps = {n: sb(n + "_var_eps", [P, G]) for n in NORMS}
        rstd = {n: sb(n + "_rstd", [P, G]) for n in NORMS}

        bank = [[ctx.enter_context(nc.psum_tensor(f"layer{l}_{b}", [P, 512], F32)) for b in range(2)]
                for l in range(LAYERS)]

        consts_in, ident_zero, ident_made, consts_set = map(sem, ("consts_in", "ident_zero", "ident_made", "consts_set"))
        weights_turned, weights_kept, gamma_in, split_hi, split_lo, shifts_made, bias_summed, setup_done = map(
            sem, ("weights_turned", "weights_kept", "gamma_in", "split_hi", "split_lo", "shifts_made", "bias_summed",
                  "setup_done"))
        x_loaded, adj_loaded, y_stored = signal("x_loaded", 16), signal("adj_loaded", 16), signal("y_stored", 16)
        adjT_ps, ax_ps, h1_ps, s2_ps, as2_ps, s3_ps, gcn_ps = (
            signal(n) for n in ("adjT_ps", "ax_ps", "h1_ps", "s2_ps", "as2_ps", "s3_ps", "gcn_ps"))
        k_ps, kx_ps, hyp2_ps = (signal(n) for n in ("k_ps", "kx_ps", "hyp2_ps"))
        hyp1_ps, kz_ps = signal("hyp1_ps", 2), signal("kz_ps", 2)
        x2T_ps, ak_ps, score_ps, prob_ps = (signal(n) for n in ("x2T_ps", "ak_ps", "score_ps", "prob_ps"))
        qkv_ps = signal("qkv_ps", 2)
        x3T_ps, s_ps, s_row_ps, y0_ps, sum_ps, hop1_ps, hop2_ps = (
            signal(n) for n in ("x3T_ps", "s_ps", "s_row_ps", "y0_ps", "sum_ps", "hop1_ps", "hop2_ps"))
        y12_ps = signal("y12_ps", 2)
        adjT_sb, ax_hi, s2_sb, s3_sb, k_sb, kx_hi, x2T_hi, x3T_hi, y0_raw = (
            signal(n) for n in (
                "adjT_sb", "ax_hi", "s2_sb", "s3_sb", "k_sb", "kx_hi", "x2T_hi", "x3T_hi", "y0_raw"))
        h1_sb, h2_sb, kz_hi, qkv_sb, y12_sb, relu_sb = (
            signal(n, 2) for n in ("h1_sb", "h2_sb", "kz_hi", "qkv_sb", "y12_sb", "relu_sb"))
        edge_exp, prob_exp = signal("edge_exp", 4), signal("prob_exp")
        ax_lo, kx_lo, x2T_lo, x3T_lo, kz_lo = (
            signal("ax_lo"), signal("kx_lo"), signal("x2T_lo"), signal("x3T_lo"), signal("kz_lo", 2))
        inc_made = signal("inc_made", 2)
        size_floor, size_inv, deg_rhs_set = signal("size_floor"), signal("size_inv"), signal("deg_rhs_set", 2)
        incw_made = signal("incw_made", 2)
        deg_prep, deg_recip, deg_done = signal("deg_prep", 2), signal("deg_recip"), signal("deg_done", 2)
        hyp1_pre = signal("hyp1_pre", 2)
        r1_based = signal("r1_based", 2)
        scored, max_found, sum_inverted, prob_normed, prob_sb = (
            signal("scored", 2), signal("max_found"), signal("sum_inverted"), signal("prob_normed"), signal("prob_sb"))
        s_sb, s02_sb, e_maxed, y0_sb, rsum_eps, rsum_inv, hop1_sb, hop2_sb = (
            signal("s_sb", 2), signal("s02_sb"), signal("e_maxed"), signal("y0_sb"),
            signal("rsum_eps"), signal("rsum_inv"), signal("hop1_sb", 2), signal("hop2_sb", 2))
        summed = {n: signal(n + "_summed", 1 if n in ("ln0", "ln3") else 2) for n in NORMS if n != "lnh"}
        stated = {n: signal(n + "_stated", 2) for n in NORMS}
        gap_taken = {n: signal(n + "_gap_taken", 2) for n in NORMS}
        gap_used = {n: signal(n + "_gap_used", 2) for n in NORMS}
        averaged = {n: signal(n + "_averaged") for n in NORMS}
        normed = {n: signal(n + "_normed", 2) for n in NORMS}
        rooted = {n: signal(n + "_rooted") for n in NORMS}
        shifted = {n: signal(n + "_shifted") for n in NORMS}
        x_b3_made, xx_half, xx_made = (signal(n) for n in ("x_b3_made", "xx_half", "xx_made"))
        alpha_made = signal("alpha_made", 2)
        adj1_kept, adj2_kept, adj3_kept, x3_copied = (
            signal(n, 16) for n in ("adj1_kept", "adj2_kept", "adj3_kept", "x3_copied"))

        def later(pair):
            return not (isinstance(pair, int) and pair == 0)

        def all_steps(eng, step):
            for t in range(STAGES):
                step(t, range(t + 1))
            with eng.Fori(STAGES, PAIRS) as t:
                step(t, range(STAGES))
            for t in range(PAIRS, PAIRS + STAGES - 1):
                step(t, range(t - PAIRS + 1, STAGES))

        const_dmas = []

        def const(dst, src):
            const_dmas.append((dst, src))

        for dst, src in ((w1_raw, gcn_w1), (w2, gcn_w2), (w3, gcn_w3), (hyp_w1_nat, hyp_w1), (hyp_w2_nat, hyp_w2),
                         (wv_nat, att_wv), (dif_wv_nat, dif_wv)):
            const(dst[:], src.rearrange("(c p) n -> p c n", p=P))
        const(wqk_nat[:], att_wqk)
        for k in range(HOPS):
            const(w_hop_raw[:, :, k, :], dif_wk[k].rearrange("(c p) n -> p c n", p=P))
            const(bk_rows[:, k, :], dif_bk[k].partition_broadcast(P))
        for g in range(G):
            const(b3_rows[:, g, :], gcn_b3.partition_broadcast(P))
            const(hyp_b2_rows[:, g, :], hyp_b2.partition_broadcast(P))
        const(hyp_b1_rows[:], hyp_b1.partition_broadcast(P))
        const(ab_col[:], dif_ab.partition_broadcast(P))
        for dst, src, n in ((b1_col, gcn_b1, FC), (b2_col, gcn_b2, FC), (gamma_col, hyp_gamma, HC),
                            (beta_col, hyp_beta, HC), (bv_col, dif_bv, FC)):
            for c in range(n):
                const(dst[:, c:c + 1], src[c * P:(c + 1) * P].rearrange("(p a) -> p a", a=1))
        for h in range(2):
            for c in range(FC):
                at = h * F + c * P
                const(aw_cols[:, h, c:c + 1], dif_aw[at:at + P, :])
        CONSTS = 16 * len(const_dmas)
        SETUP = 7

        block = ctx.enter_context(nc.Block())

        @block.sync
        def _(sp):
            for dst, src in const_dmas:
                sp.dma_start(dst, src).then_inc(consts_in, 16)

            def load(t):
                if later(t):
                    sp.wait_ge(adjT_ps.sem, adjT_ps.at(t - 1))
                sp.dma_start(adj_in[:], adj_pairs[t]).then_inc(adj_loaded.sem, 16)
                if later(t):
                    sp.wait_ge(ax_ps.sem, ax_ps.at(t - 1))
                    sp.wait_ge(x_b3_made.sem, x_b3_made.at(t - 1))
                sp.dma_start(x_in[:], x_pairs[t]).then_inc(x_loaded.sem, 16)

            def step(t, on):
                p0, p1, p2, p3, p4 = t, t - 1, t - 2, t - 3, t - 4
                if 3 in on:
                    if 4 in on:
                        sp.wait_ge(summed["ln3"].sem, summed["ln3"].at(p4))
                    sp.wait_ge(normed["ln2"].sem, normed["ln2"].at(p3))
                    sp.dma_start(x3_kept[:], x3[:]).then_inc(x3_copied.sem, 16)
                if 0 in on and not (isinstance(p0, int) and p0 == PAIRS - 1):
                    load(p0 + 1)
                if 4 in on:
                    sp.wait_ge(normed["ln3"].sem, normed["ln3"].at(p4))
                    sp.dma_start(out_pairs[p4], y_out[:]).then_inc(y_stored.sem, 16)
                if 2 in on:
                    sp.wait_ge(ak_ps.sem, ak_ps.at(p2))
                    if 3 in on:
                        sp.wait_ge(alpha_made.sem, alpha_made.at(p3))
                    sp.dma_start(adjT3[:], adjT2[:]).then_inc(adj3_kept.sem, 16)
                if 1 in on:
                    if 2 in on:
                        sp.wait_ge(adj3_kept.sem, adj3_kept.at(p2))
                    sp.wait_ge(adj1_kept.sem, adj1_kept.at(p1))
                    sp.dma_start(adjT2[:], adjT1[:]).then_inc(adj2_kept.sem, 16)
                if 0 in on:
                    sp.wait_ge(gcn_ps.sem, gcn_ps.at(p0))
                    sp.wait_ge(deg_rhs_set.sem, deg_rhs_set.at(p0))
                    if 1 in on:
                        sp.wait_ge(adj2_kept.sem, adj2_kept.at(p1))
                    sp.dma_start(adjT1[:], adjT0[:]).then_inc(adj1_kept.sem, 16)

            load(0)
            for t in range(STAGES):
                step(t, range(t + 1))
            with sp.Fori(STAGES, PAIRS - 1) as t:
                step(t, range(STAGES))
            for t in range(PAIRS - 1, PAIRS + STAGES - 1):
                step(t, range(max(0, t - PAIRS + 1), STAGES))
            sp.wait_ge(y_stored.sem, y_stored.at(PAIRS - 1))

        @block.tensor
        def _(pe):
            mm, turn = nc.tensor.matmul, nc.tensor.transpose
            everything = bank[0] + bank[1] + bank[2] + bank[3]

            pe.wait_ge(consts_in, CONSTS)
            pe.wait_ge(ident_made, 1)
            for c in range(FC):
                for h in range(HC):
                    turn(everything[c][:, h * P:(h + 1) * P], hyp_w1_nat[:, h, c * P:(c + 1) * P], ident[:])
            for h in range(HC):
                for o in range(FC):
                    at = (h % 2) * F + o * P
                    turn(everything[2 + h // 2][:, at:at + P], hyp_w2_nat[:, o, h * P:(h + 1) * P], ident[:])
            for c in range(FC):
                turn(everything[4 + c][:, 0:QK], wqk_nat[:, c * P:(c + 1) * P], ident[:])
                for o in range(FC):
                    turn(everything[4 + c][:, QK + o * P:QK + (o + 1) * P], wv_nat[:, o, c * P:(c + 1) * P], ident[:])
            for o in range(FC):
                for c in range(FC):
                    last = turn(everything[6][:, o * F + c * P:o * F + (c + 1) * P],
                                dif_wv_nat[:, c, o * P:(o + 1) * P], ident[:])
            last.then_inc(weights_turned, 1)
            pe.wait_ge(weights_kept, 3)
            for h in range(HC):
                mm(everything[7][:, 0:F], beta_col[:, h:h + 1].to_broadcast([P, P]), hyp_w2T[:, h, :],
                   start=(h == 0), stop=(h == HC - 1))
            for c in range(FC):
                for o in range(FC):
                    mm(everything[7][:, F + 2 * c:F + 2 * c + 2], dif_wvT[:, o, c * P:(c + 1) * P], aw_cols[:, :, o],
                       start=(o == 0), stop=(o == FC - 1))
            for o in range(FC):
                last = mm(everything[7][:, F + 8:F + 10], bv_col[:, o:o + 1].to_broadcast([P, P]), aw_cols[:, :, o],
                          start=(o == 0), stop=(o == FC - 1))
            last.then_inc(shifts_made, 1)
            pe.wait_ge(consts_set, 2)
            pe.wait_ge(setup_done, SETUP)

            def turn_x(dst, src):
                for c in range(FC):
                    for g in range(G):
                        at = (c * G + g) * N
                        last = turn(dst[:, at:at + N], src[:, g, c * P:(c + 1) * P], ident[:])
                return last

            def nodes_mix(dst, src, mix):
                for c in range(FC):
                    for g in range(G):
                        at = (c * G + g) * N
                        last = mm(dst[:, at:at + N], src[:, g, c * P:(c + 1) * P], mix[:, g, :], start=True, stop=True)
                return last

            def mm3(dst, lhsT, rhs, start, stop):
                mm(dst, lhsT[0], rhs[0], start=start, stop=False)
                mm(dst, lhsT[0], rhs[1], start=False, stop=False)
                return mm(dst, lhsT[1], rhs[0], start=False, stop=stop)

            def part(pair, *at):
                return pair[0][at], pair[1][at]

            ALL = slice(None)

            def weigh3(dst, srcT, w):
                for g in range(G):
                    for c in range(FC):
                        last = mm3(dst[:, g * F:(g + 1) * F], part(srcT, ALL, c, g, ALL), part(w, ALL, c, ALL),
                                   start=(c == 0), stop=(c == FC - 1))
                return last

            def hop_weights(k):
                return tuple(h[:, :, k, :] for h in w_hop)

            def weigh(dst, srcT, w):
                for g in range(G):
                    for c in range(FC):
                        last = mm(dst[:, g * F:(g + 1) * F], srcT[:, c, g, :], w[:, c, :],
                                  start=(c == 0), stop=(c == FC - 1))
                return last

            def step(t, on):
                p0, p1, p2, p3, p4 = t, t - 1, t - 2, t - 3, t - 4
                if 3 in on:
                    pe.wait_ge(normed["ln2"].sem, normed["ln2"].at(p3))
                    if later(p3):
                        pe.wait_ge(hop1_sb.sem, hop1_sb.at(p3 - 1))
                    turn_x(bank[3][0], x3).then_inc(x3T_ps.sem, 1)
                if 1 in on:
                    pe.wait_ge(incw_made.sem, incw_made.at(p1))
                    pe.wait_ge(deg_rhs_set.sem, deg_rhs_set.at(p1))
                    if later(p1):
                        pe.wait_ge(kz_lo.sem, kz_lo.at(p1 - 1, 1))
                    for g in range(G):
                        mm(bank[1][1][:, g * N:(g + 1) * N], incT[:, g, :], incT_w[:, g, :], start=True, stop=True)
                    for g in range(G):
                        last = mm(bank[1][1][:, G * N + 2 * g:G * N + 2 * g + 2], incT[:, g, :], deg_rhs[:, g, :],
                                  start=True, stop=True)
                    last.then_inc(k_ps.sem, 1)
                if 0 in on:
                    pe.wait_ge(adj_loaded.sem, adj_loaded.at(p0))
                    if later(p0):
                        pe.wait_ge(summed["ln0"].sem, summed["ln0"].at(p0 - 1))
                    for g in range(G):
                        last = turn(bank[0][0][:, g * N:(g + 1) * N], adj_in[:, g, :], ident[:])
                    last.then_inc(adjT_ps.sem, 1)
                if 1 in on:
                    pe.wait_ge(k_sb.sem, k_sb.at(p1))
                    pe.wait_ge(normed["ln0"].sem, normed["ln0"].at(p1))
                    if later(p1):
                        pe.wait_ge(summed["ln1"].sem, summed["ln1"].at(p1 - 1))
                    nodes_mix(bank[1][0], x1, kmat).then_inc(kx_ps.sem, 1)
                if 0 in on:
                    pe.wait_ge(adjT_sb.sem, adjT_sb.at(p0))
                    pe.wait_ge(x_loaded.sem, x_loaded.at(p0))
                    if later(p0):
                        pe.wait_ge(s3_sb.sem, s3_sb.at(p0 - 1))
                    nodes_mix(bank[0][1], x_in, adjT0).then_inc(ax_ps.sem, 1)
                if 3 in on:
                    pe.wait_ge(x3T_lo.sem, x3T_lo.at(p3))
                    if later(p3):
                        pe.wait_ge(hop2_sb.sem, hop2_sb.at(p3 - 1))
                    for g in range(G):
                        for c in range(FC):
                            last = mm3(bank[3][1][:, 2 * g:2 * g + 2], part(x3T, ALL, c, g, ALL), part(wa, ALL, c, ALL),
                                       start=(c == 0), stop=(c == FC - 1))
                    last.then_inc(s_ps.sem, 1)
                if 1 in on:
                    pe.wait_ge(kx_lo.sem, kx_lo.at(p1))
                    for g in range(G):
                        for c in range(FC):
                            last = mm3(bank[1][1 - g][:, 0:DH], part(kxT, ALL, c, g, ALL), part(hyp_w1T, ALL, c, ALL),
                                       start=(c == 0), stop=(c == FC - 1))
                        last.then_inc(hyp1_ps.sem, 1)
                if 2 in on:
                    pe.wait_ge(normed["ln1"].sem, normed["ln1"].at(p2))
                    if later(p2):
                        pe.wait_ge(prob_sb.sem, prob_sb.at(p2 - 1))
                    turn_x(bank[2][0], x2).then_inc(x2T_ps.sem, 1)
                if 0 in on:
                    pe.wait_ge(ax_lo.sem, ax_lo.at(p0))
                    for h in range(FC):
                        for c in range(FC):
                            last = mm3(bank[0][0][:, h * G * N:(h + 1) * G * N], part(w1, ALL, c, slice(h * P, (h + 1) * P)),
                                       part(axT, ALL, c, ALL, ALL), start=(c == 0), stop=(c == FC - 1))
                    last.then_inc(h1_ps.sem, 1)
                if 3 in on:
                    pe.wait_ge(s_sb.sem, s_sb.at(p3))
                    for g in range(G):
                        last = turn(bank[3][0][:, g * N:(g + 1) * N], s_cols[:, g, 1:2].to_broadcast([P, P]), ident[:])
                    last.then_inc(s_row_ps.sem, 1)
                if 2 in on:
                    pe.wait_ge(x2T_lo.sem, x2T_lo.at(p2))
                    for g in range(G):
                        for c in range(FC):
                            last = mm3(bank[2][1 - g][:, 0:QKV], part(x2T, ALL, c, g, ALL), part(w_qkv, ALL, c, ALL),
                                       start=(c == 0), stop=(c == FC - 1))
                        last.then_inc(qkv_ps.sem, 1)
                if 0 in on:
                    pe.wait_ge(h1_sb.sem, h1_sb.at(p0))
                    weigh(bank[0][1], h1T, w2).then_inc(s2_ps.sem, 1)
                if 3 in on:
                    weigh3(bank[3][1], x3T, hop_weights(1)).then_inc(y12_ps.sem, 1)
                    pe.wait_ge(edge_exp.sem, edge_exp.at(p3))
                    weigh3(bank[3][0], x3T, hop_weights(2)).then_inc(y12_ps.sem, 1)
                if 2 in on:
                    pe.wait_ge(qkv_sb.sem, qkv_sb.at(p2))
                    pe.wait_ge(adj2_kept.sem, adj2_kept.at(p2))
                    for g in range(G):
                        last = mm(bank[2][1][:, g * DA:(g + 1) * DA], adjT2[:, g, :], qkv[:, g, DA:2 * DA],
                                  start=True, stop=True)
                    last.then_inc(ak_ps.sem, 1)
                if 0 in on:
                    pe.wait_ge(s2_sb.sem, s2_sb.at(p0))
                    nodes_mix(bank[0][0], s2, adjT0).then_inc(as2_ps.sem, 1)
                if 1 in on:
                    for g in range(G):
                        pe.wait_ge(normed["lnh"].sem, normed["lnh"].at(p1, g + 1))
                        for h in range(HC):
                            last = mm(bank[1][1 - g][:, h * N:(h + 1) * N], z[:, g, h * P:(h + 1) * P], kmat[:, g, :],
                                      start=True, stop=True)
                        last.then_inc(kz_ps.sem, 1)
                if 2 in on:
                    pe.wait_ge(scored.sem, scored.at(p2))
                    mm(bank[2][0][0:G, 0:N], score[:], ident[:], start=True, stop=True).then_inc(score_ps.sem, 1)
                if 0 in on:
                    pe.wait_ge(h2_sb.sem, h2_sb.at(p0))
                    weigh(bank[0][1], h2T, w3).then_inc(s3_ps.sem, 1)
                if 3 in on:
                    pe.wait_ge(y12_sb.sem, y12_sb.at(p3, 1))
                    weigh3(bank[3][1], x3T, hop_weights(0)).then_inc(y0_ps.sem, 1)
                if 2 in on:
                    pe.wait_ge(prob_normed.sem, prob_normed.at(p2))
                    mm(bank[2][0][:, 0:G], prob_row[:], ident[0:G, 0:G], start=True, stop=True).then_inc(prob_ps.sem, 1)
                if 3 in on:
                    pe.wait_ge(y12_sb.sem, y12_sb.at(p3))
                    pe.wait_ge(alpha_made.sem, alpha_made.at(p3))
                    for g in range(G):
                        last = mm(bank[3][0][:, g:g + 1], alphaT[:, g, :], ones[:], start=True, stop=True)
                    last.then_inc(sum_ps.sem, 1)
                if 0 in on:
                    pe.wait_ge(s3_sb.sem, s3_sb.at(p0))
                    for g in range(G):
                        last = mm(bank[0][0][:, g * F:(g + 1) * F], adjT0[:, g, :], s3[:, g, :], start=True, stop=True)
                    last.then_inc(gcn_ps.sem, 1)
                if 3 in on:
                    pe.wait_ge(rsum_eps.sem, rsum_eps.at(p3))
                    for g in range(G):
                        last = mm(bank[3][0][:, g * F:(g + 1) * F], alphaT[:, g, :], y2[:, g, :], start=True, stop=True)
                    last.then_inc(hop1_ps.sem, 1)
                if 1 in on:
                    pe.wait_ge(kz_lo.sem, kz_lo.at(p1))
                    for g in range(G):
                        for h in range(HC):
                            last = mm3(bank[1][0][:, g * F:(g + 1) * F], part(kzT, ALL, g, h, ALL), part(hyp_w2g, ALL, h, ALL),
                                       start=(h == 0), stop=(h == HC - 1))
                    last.then_inc(hyp2_ps.sem, 1)
                if 3 in on:
                    pe.wait_ge(hop1_sb.sem, hop1_sb.at(p3))
                    pe.wait_ge(y0_raw.sem, y0_raw.at(p3))
                    for g in range(G):
                        last = mm(bank[3][1][:, g * F:(g + 1) * F], alphaT[:, g, :], hop1[:, g, :],
                                  start=True, stop=True)
                    last.then_inc(hop2_ps.sem, 1)

            all_steps(pe, step)

        @block.scalar
        def _(act):
            def copy(dst, src):
                return nc.scalar.activation(dst, src, ACT.Copy)

            def flat(a):
                return a[:].rearrange("p a b c -> p (a b c)") if len(a.shape) == 4 else a[:].rearrange("p a b -> p (a b)")

            def normalise(n, p, dst, src):
                act.wait_ge(shifted[n].sem, shifted[n].at(p))
                for g in range(G):
                    nc.scalar.activation(dst[:, g, :], src[:, g, :], ACT.Identity, bias=shift[n][:, g:g + 1],
                                         scale=rstd[n][:, g:g + 1]).then_inc(normed[n].sem, 1)

            def step(t, on):
                p0, p1, p2, p3, p4 = t, t - 1, t - 2, t - 3, t - 4
                if 3 in on:
                    act.wait_ge(x3T_ps.sem, x3T_ps.at(p3))
                    copy(flat(x3T[0]), bank[3][0][:]).then_inc(x3T_hi.sem, 1)
                if 1 in on:
                    act.wait_ge(k_ps.sem, k_ps.at(p1))
                    if later(p1):
                        act.wait_ge(deg_done.sem, deg_done.at(p1 - 1))
                    copy(kdeg[:], bank[1][1][:, 0:G * N + 2 * G]).then_inc(k_sb.sem, 1)
                if 0 in on:
                    act.wait_ge(adjT_ps.sem, adjT_ps.at(p0))
                    if later(p0):
                        act.wait_ge(adj1_kept.sem, adj1_kept.at(p0 - 1))
                    copy(flat(adjT0), bank[0][0][:, 0:G * N]).then_inc(adjT_sb.sem, 1)
                if 1 in on:
                    act.wait_ge(kx_ps.sem, kx_ps.at(p1))
                    copy(flat(kxT[0]), bank[1][0][:]).then_inc(kx_hi.sem, 1)
                if 2 in on:
                    normalise("ln1", p2, x2, r1)
                if 0 in on:
                    act.wait_ge(ax_ps.sem, ax_ps.at(p0))
                    copy(flat(axT[0]), bank[0][1][:]).then_inc(ax_hi.sem, 1)
                if 1 in on:
                    for g in range(G):
                        act.wait_ge(hyp1_pre.sem, hyp1_pre.at(p1, g + 1))
                        if later(p1):
                            act.wait_ge(normed["lnh"].sem, normed["lnh"].at(p1 - 1, g + 1))
                        nc.scalar.activation(h_act[:, g, :], h_pre[:, g, :], ACT.Relu).then_inc(relu_sb.sem, 1)
                if 2 in on:
                    act.wait_ge(x2T_ps.sem, x2T_ps.at(p2))
                    copy(flat(x2T[0]), bank[2][0][:]).then_inc(x2T_hi.sem, 1)
                if 0 in on:
                    act.wait_ge(h1_ps.sem, h1_ps.at(p0))
                    for c in range(FC):
                        nc.scalar.activation(h1T[:, c, :, :], bank[0][0][:, c * G * N:(c + 1) * G * N], ACT.Relu,
                                             bias=b1_col[:, c:c + 1]).then_inc(h1_sb.sem, 1)
                if 3 in on:
                    act.wait_ge(s_row_ps.sem, s_row_ps.at(p3))
                    act.wait_ge(s02_sb.sem, s02_sb.at(p3))
                    if later(p3):
                        act.wait_ge(e_maxed.sem, e_maxed.at(p3 - 1))
                    for g in range(G):
                        row = bank[3][0][:, g * N:(g + 1) * N]
                        nc.scalar.activation(e_pos[:, g, :], row, ACT.Exp,
                                             bias=s_cols[:, g, 0:1]).then_inc(edge_exp.sem, 1)
                        nc.scalar.activation(e_neg[:, g, :], row, ACT.Exp, scale=0.2,
                                             bias=s_col02[:, g:g + 1]).then_inc(edge_exp.sem, 1)
                if 2 in on:
                    for g in range(G):
                        act.wait_ge(qkv_ps.sem, qkv_ps.at(p2, g + 1))
                        if later(p2):
                            act.wait_ge(summed["ln2"].sem, summed["ln2"].at(p2 - 1))
                        copy(qkv[:, g, :], bank[2][1 - g][:, 0:QKV]).then_inc(qkv_sb.sem, 1)
                if 0 in on:
                    act.wait_ge(s2_ps.sem, s2_ps.at(p0))
                    copy(flat(s2), bank[0][1][:]).then_inc(s2_sb.sem, 1)
                if 4 in on:
                    if later(p4):
                        act.wait_ge(y_stored.sem, y_stored.at(p4 - 1))
                    normalise("ln3", p4, y_out, r3)
                if 3 in on:
                    act.wait_ge(y12_ps.sem, y12_ps.at(p3, 1))
                    copy(flat(y1), bank[3][1][:]).then_inc(y12_sb.sem, 1)
                    act.wait_ge(y12_ps.sem, y12_ps.at(p3, 2))
                    copy(flat(y2), bank[3][0][:]).then_inc(y12_sb.sem, 1)
                if 0 in on:
                    act.wait_ge(as2_ps.sem, as2_ps.at(p0))
                    for c in range(FC):
                        nc.scalar.activation(h2T[:, c, :, :], bank[0][0][:, c * G * N:(c + 1) * G * N], ACT.Relu,
                                             bias=b2_col[:, c:c + 1]).then_inc(h2_sb.sem, 1)
                if 1 in on:
                    for g in range(G):
                        act.wait_ge(kz_ps.sem, kz_ps.at(p1, g + 1))
                        copy(kzT[0][:, g, :, :].rearrange("p h n -> p (h n)"),
                             bank[1][1 - g][:]).then_inc(kz_hi.sem, 1)
                if 2 in on:
                    act.wait_ge(max_found.sem, max_found.at(p2))
                    if later(p2):
                        act.wait_ge(prob_normed.sem, prob_normed.at(p2 - 1))
                    nc.scalar.activation(prob_e[:], bank[2][0][0:G, 0:N], ACT.Exp, bias=neg_max[:],
                                         accum_out=prob_sum[:]).then_inc(prob_exp.sem, 1)
                if 0 in on:
                    act.wait_ge(s3_ps.sem, s3_ps.at(p0))
                    copy(flat(s3), bank[0][1][:]).then_inc(s3_sb.sem, 1)
                if 3 in on:
                    act.wait_ge(y0_ps.sem, y0_ps.at(p3))
                    if later(p3):
                        act.wait_ge(y0_sb.sem, y0_sb.at(p3 - 1))
                    copy(flat(y0_plain), bank[3][1][:]).then_inc(y0_raw.sem, 1)
                if 2 in on:
                    if 3 in on:
                        act.wait_ge(x3_copied.sem, x3_copied.at(p3))
                    normalise("ln2", p2, x3, r2)
                if 0 in on:
                    normalise("ln0", p0, x1, r0)

            act.wait_ge(consts_in, CONSTS)
            all_steps(act, step)

        @block.vector
        def _(dve):
            v = nc.vector
            everything = bank[0] + bank[1] + bank[2] + bank[3]

            def split(pair, src):
                v.tensor_copy(pair[0], src).then_inc(split_hi, 1)
                splits[0] += 1
                dve.wait_ge(split_hi, splits[0])
                v.tensor_tensor(pair[1], src, pair[0].bitcast(F32), ALU.subtract).then_inc(split_lo, 1)

            splits = [0]

            def rows(pair, c):
                return pair[0][:, c, :], pair[1][:, c, :]

            def whole(pair):
                form = "p a b -> p (a b)" if len(pair[0].shape) == 3 else "p a b c -> p (a b c)"
                return pair[0][:].rearrange(form), pair[1][:].rearrange(form)

            dve.wait_ge(weights_turned, 1)
            for b in range(2):
                v.tensor_copy(hyp_w2T[:, 2 * b:2 * b + 2, :].rearrange("p a b -> p (a b)"),
                              everything[2 + b][:]).then_inc(weights_kept, 1)
            v.tensor_copy(dif_wvT[:].rearrange("p a b -> p (a b)"), everything[6][:]).then_inc(weights_kept, 1)
            for c in range(FC):
                split(rows(hyp_w1T, c), everything[c][:])
            for c in range(FC):
                split(rows(w_qkv, c), everything[4 + c][:, 0:QKV])
            dve.wait_ge(consts_in, CONSTS)
            split(whole(w1), w1_raw[:].rearrange("p a b -> p (a b)"))
            split(whole(w_hop), w_hop_raw[:].rearrange("p a b c -> p (a b c)"))
            dve.wait_ge(weights_kept, 3)
            for h in range(HC):
                v.tensor_scalar(hyp_w2g_raw[:, h, :], hyp_w2T[:, h, :], gamma_col[:, h:h + 1], None,
                                ALU.mult).then_inc(gamma_in, 1)
            v.tensor_tensor(bk_tmp[:], bk_rows[:, 0, :], bk_rows[:, 1, :], ALU.add).then_inc(bias_summed, 1)
            dve.wait_ge(gamma_in, HC)
            split(whole(hyp_w2g), hyp_w2g_raw[:].rearrange("p a b -> p (a b)"))
            dve.wait_ge(bias_summed, 1)
            for g in range(G):
                v.tensor_tensor(bk_sum[:, g, :], bk_tmp[:], bk_rows[:, 2, :], ALU.add).then_inc(setup_done, 1)
            dve.wait_ge(shifts_made, 1)
            v.tensor_copy(hyp_shift[:], everything[7][:, 0:F]).then_inc(setup_done, 1)
            v.tensor_copy(wa_raw[:].rearrange("p a b -> p (a b)"), everything[7][:, F:F + 2 * FC]).then_inc(setup_done, 1)
            v.tensor_copy(s_part[:], everything[7][:, F + 8:F + 10]).then_inc(setup_done, 1)
            dve.wait_ge(setup_done, 5)
            split(whole(wa), wa_raw[:].rearrange("p a b -> p (a b)"))
            v.tensor_tensor(s_const[:], s_part[:, 0:1], s_part[:, 1:2], ALU.add).then_inc(setup_done, 1)
            dve.wait_ge(setup_done, 6)
            v.tensor_tensor(s_const[:], s_const[:], ab_col[:], ALU.add).then_inc(setup_done, 1)
            dve.wait_ge(setup_done, SETUP)
            dve.wait_ge(split_lo, splits[0])
            dve.wait_ge(consts_set, 2)

            def trailing(done, dst, src, hi):
                v.tensor_tensor(dst, src, hi.bitcast(F32), ALU.subtract).then_inc(done.sem, 1)

            def flat(a):
                return a[:].rearrange("p a b c -> p (a b c)") if len(a.shape) == 4 else a[:].rearrange("p a b -> p (a b)")

            def statistics(n, p, src, ready):
                for g in range(G):
                    ready(g)
                    v.bn_stats(stats[n][:, g, :], src[:, g, :]).then_inc(stated[n].sem, 1)
                half_mean = stats[n][:, :, 1::3]
                half_sum = stats[n][:, :, 2::3]
                size = src.shape[2]
                dve.wait_ge(stated[n].sem, stated[n].at(p))
                v.tensor_tensor(mean_gap[n][:], half_mean[:, :, 0], half_mean[:, :, 1], ALU.subtract)\
                    .then_inc(gap_taken[n].sem, 1)
                v.scalar_tensor_tensor(square_sum[n][:], half_sum[:, :, 0], EPS * size, half_sum[:, :, 1],
                                       ALU.add, ALU.add).then_inc(gap_taken[n].sem, 1)
                dve.wait_ge(gap_taken[n].sem, gap_taken[n].at(p, 1))
                v.scalar_tensor_tensor(neg_mean[n][:], mean_gap[n][:], 0.5, half_mean[:, :, 0],
                                       ALU.mult, ALU.subtract).then_inc(gap_used[n].sem, 1)
                v.scalar_tensor_tensor(gap_square[n][:], mean_gap[n][:], 0.25, mean_gap[n][:],
                                       ALU.mult, ALU.mult).then_inc(gap_used[n].sem, 1)
                dve.wait_ge(gap_used[n].sem, gap_used[n].at(p))
                v.scalar_tensor_tensor(var_eps[n][:], square_sum[n][:], 1.0 / size, gap_square[n][:],
                                       ALU.mult, ALU.add).then_inc(averaged[n].sem, 1)

            def normalise(n, p, dst, src):
                dve.wait_ge(rooted[n].sem, rooted[n].at(p))
                for g in range(G):
                    v.tensor_scalar(dst[:, g, :], src[:, g, :], neg_mean[n][:, g:g + 1], rstd[n][:, g:g + 1],
                                    ALU.add, ALU.mult).then_inc(normed[n].sem, 1)

            def step(t, on):
                p0, p1, p2, p3, p4 = t, t - 1, t - 2, t - 3, t - 4
                if 3 in on:
                    dve.wait_ge(x3T_hi.sem, x3T_hi.at(p3))
                    trailing(x3T_lo, flat(x3T[1]), bank[3][0][:], flat(x3T[0]))
                if 1 in on:
                    dve.wait_ge(k_sb.sem, k_sb.at(p1))
                    v.tensor_scalar(deg_pos[:], deg[:, :, 1], 0.0, None, ALU.is_gt).then_inc(deg_prep.sem, 1)
                    v.tensor_scalar(deg_safe[:], deg[:, :, 1], TINY, None, ALU.max).then_inc(deg_prep.sem, 1)
                    dve.wait_ge(deg_prep.sem, deg_prep.at(p1))
                    v.reciprocal(deg_rec[:], deg_safe[:]).then_inc(deg_recip.sem, 1)
                    dve.wait_ge(deg_recip.sem, deg_recip.at(p1))
                    v.tensor_tensor(deg_inv[:], deg_rec[:], deg_pos[:], ALU.mult).then_inc(deg_done.sem, 1)
                    dve.wait_ge(deg_done.sem, deg_done.at(p1, 1))
                    v.tensor_tensor(row_sum[:], deg_inv[:], deg[:, :, 0], ALU.mult).then_inc(deg_done.sem, 1)
                    dve.wait_ge(kx_hi.sem, kx_hi.at(p1))
                    trailing(kx_lo, flat(kxT[1]), bank[1][0][:], flat(kxT[0]))
                if 0 in on:
                    dve.wait_ge(ax_hi.sem, ax_hi.at(p0))
                    trailing(ax_lo, flat(axT[1]), bank[0][1][:], flat(axT[0]))
                if 3 in on:
                    dve.wait_ge(s_ps.sem, s_ps.at(p3))
                    s_view = bank[3][1][:, 0:2 * G].rearrange("p (g j) -> p g j", j=2)
                    v.tensor_scalar(s_cols[:, :, 0], s_view[:, :, 0], s_const[:], None, ALU.add).then_inc(s_sb.sem, 1)
                    v.tensor_copy(s_cols[:, :, 1], s_view[:, :, 1]).then_inc(s_sb.sem, 1)
                    dve.wait_ge(s_sb.sem, s_sb.at(p3, 1))
                    v.tensor_scalar(s_col02[:], s_cols[:, :, 0], 0.2, None, ALU.mult).then_inc(s02_sb.sem, 1)
                if 1 in on:
                    for g in range(G):
                        dve.wait_ge(hyp1_ps.sem, hyp1_ps.at(p1, g + 1))
                        dve.wait_ge(deg_done.sem, deg_done.at(p1))
                        v.scalar_tensor_tensor(h_pre[:, g, :], bank[1][1 - g][:, 0:DH], deg_inv[:, g:g + 1],
                                               hyp_b1_rows[:], ALU.mult, ALU.add).then_inc(hyp1_pre.sem, 1)
                if 2 in on:
                    dve.wait_ge(x2T_hi.sem, x2T_hi.at(p2))
                    trailing(x2T_lo, flat(x2T[1]), bank[2][0][:], flat(x2T[0]))
                if 1 in on:
                    statistics("lnh", p1, h_act, lambda g: dve.wait_ge(relu_sb.sem, relu_sb.at(p1, g + 1)))
                if 4 in on:
                    dve.wait_ge(hop2_sb.sem, hop2_sb.at(p4))
                    dve.wait_ge(x3_copied.sem, x3_copied.at(p4))
                    v.scalar_tensor_tensor(flat(r3), flat(hop2), 0.0, flat(x3_kept), ALU.max, ALU.add)\
                        .then_inc(summed["ln3"].sem, 1)
                    statistics("ln3", p4, r3, lambda g: dve.wait_ge(summed["ln3"].sem, summed["ln3"].at(p4)))
                if 3 in on:
                    dve.wait_ge(edge_exp.sem, edge_exp.at(p3))
                    if later(p3):
                        dve.wait_ge(alpha_made.sem, alpha_made.at(p3 - 1))
                    v.tensor_tensor(flat(e_max), flat(e_pos), flat(e_neg), ALU.max).then_inc(e_maxed.sem, 1)
                if 1 in on:
                    normalise("lnh", p1, z, h_act)
                    dve.wait_ge(xx_made.sem, xx_made.at(p1))
                    for g in range(G):
                        v.scalar_tensor_tensor(r1_base[:, g, :], hyp_shift[:], row_sum[:, g:g + 1], xx[:, g, :],
                                               ALU.mult, ALU.add).then_inc(r1_based.sem, 1)
                if 0 in on:
                    dve.wait_ge(adjT_sb.sem, adjT_sb.at(p0))
                    for g in range(G):
                        v.tensor_scalar(incT[:, g, :], adjT0[:, g, :], 0.0, None, ALU.not_equal, ALU.add,
                                        accum_out=edge_size[:, g:g + 1]).then_inc(inc_made.sem, 1)
                    dve.wait_ge(inc_made.sem, inc_made.at(p0))
                    v.tensor_scalar(edge_size1[:], edge_size[:], 1.0, None, ALU.max).then_inc(size_floor.sem, 1)
                    dve.wait_ge(size_floor.sem, size_floor.at(p0))
                    v.reciprocal(edge_inv[:], edge_size1[:]).then_inc(size_inv.sem, 1)
                    dve.wait_ge(size_inv.sem, size_inv.at(p0))
                    v.tensor_tensor(deg_rhs[:, :, 0], edge_inv[:], edge_size[:], ALU.mult).then_inc(deg_rhs_set.sem, 1)
                    v.tensor_copy(deg_rhs[:, :, 1], adjT0[:, :, 0]).then_inc(deg_rhs_set.sem, 1)
                    for g in range(G):
                        v.tensor_scalar(incT_w[:, g, :], incT[:, g, :], edge_inv[:, g:g + 1], None,
                                        ALU.mult).then_inc(incw_made.sem, 1)
                if 2 in on:
                    dve.wait_ge(ak_ps.sem, ak_ps.at(p2))
                    for g in range(G):
                        v.scalar_tensor_tensor(qak[:, g, :], bank[2][1][:, g * DA:(g + 1) * DA], INV_SCALE,
                                               qkv[:, g, 0:DA], ALU.mult, ALU.mult,
                                               accum_out=score[:, g:g + 1]).then_inc(scored.sem, 1)
                if 1 in on:
                    dve.wait_ge(kz_hi.sem, kz_hi.at(p1, 1))
                    trailing(kz_lo, kzT[1][:, 0, :, :].rearrange("p h n -> p (h n)"), bank[1][1][:],
                             kzT[0][:, 0, :, :].rearrange("p h n -> p (h n)"))
                if 2 in on:
                    dve.wait_ge(score_ps.sem, score_ps.at(p2))
                    v.tensor_reduce(neg_max[:], bank[2][0][0:G, 0:N], AX.X, ALU.max, negate=True).then_inc(max_found.sem, 1)
                if 1 in on:
                    dve.wait_ge(kz_hi.sem, kz_hi.at(p1, 2))
                    trailing(kz_lo, kzT[1][:, 1, :, :].rearrange("p h n -> p (h n)"), bank[1][0][:],
                             kzT[0][:, 1, :, :].rearrange("p h n -> p (h n)"))
                if 2 in on:
                    dve.wait_ge(prob_exp.sem, prob_exp.at(p2))
                    v.reciprocal(prob_inv[:], prob_sum[:]).then_inc(sum_inverted.sem, 1)
                    dve.wait_ge(sum_inverted.sem, sum_inverted.at(p2))
                    v.tensor_scalar(prob_row[:], prob_e[:], prob_inv[:], None, ALU.mult).then_inc(prob_normed.sem, 1)
                if 3 in on:
                    dve.wait_ge(sum_ps.sem, sum_ps.at(p3))
                    v.tensor_scalar(sum_eps[:], bank[3][0][:, 0:G], 1e-12, None, ALU.add).then_inc(rsum_eps.sem, 1)
                    dve.wait_ge(rsum_eps.sem, rsum_eps.at(p3))
                    v.reciprocal(sum_inv[:], sum_eps[:]).then_inc(rsum_inv.sem, 1)
                if 2 in on:
                    dve.wait_ge(prob_ps.sem, prob_ps.at(p2))
                    v.tensor_copy(prob[:], bank[2][0][:, 0:G]).then_inc(prob_sb.sem, 1)
                    dve.wait_ge(prob_sb.sem, prob_sb.at(p2))
                    for g in range(G):
                        v.scalar_tensor_tensor(r2[:, g, :], qkv[:, g, QK:QKV], prob[:, g:g + 1], x2[:, g, :],
                                               ALU.mult, ALU.add).then_inc(summed["ln2"].sem, 1)
                    statistics("ln2", p2, r2, lambda g: dve.wait_ge(summed["ln2"].sem, summed["ln2"].at(p2, g + 1)))
                if 0 in on:
                    dve.wait_ge(gcn_ps.sem, gcn_ps.at(p0))
                    dve.wait_ge(x_b3_made.sem, x_b3_made.at(p0))
                    v.tensor_tensor(flat(r0), bank[0][0][:], flat(x_b3), ALU.add).then_inc(summed["ln0"].sem, 1)
                    statistics("ln0", p0, r0, lambda g: dve.wait_ge(summed["ln0"].sem, summed["ln0"].at(p0)))
                if 3 in on:
                    dve.wait_ge(hop1_ps.sem, hop1_ps.at(p3))
                    dve.wait_ge(rsum_inv.sem, rsum_inv.at(p3))
                    for g in range(G):
                        v.scalar_tensor_tensor(hop1[:, g, :], bank[3][0][:, g * F:(g + 1) * F], sum_inv[:, g:g + 1],
                                               y1[:, g, :], ALU.mult, ALU.add).then_inc(hop1_sb.sem, 1)
                if 1 in on:
                    dve.wait_ge(hyp2_ps.sem, hyp2_ps.at(p1))
                    dve.wait_ge(r1_based.sem, r1_based.at(p1))
                    for g in range(G):
                        v.scalar_tensor_tensor(r1[:, g, :], bank[1][0][:, g * F:(g + 1) * F], deg_inv[:, g:g + 1],
                                               r1_base[:, g, :], ALU.mult, ALU.add).then_inc(summed["ln1"].sem, 1)
                    statistics("ln1", p1, r1, lambda g: dve.wait_ge(summed["ln1"].sem, summed["ln1"].at(p1, g + 1)))
                if 3 in on:
                    dve.wait_ge(hop2_ps.sem, hop2_ps.at(p3))
                    dve.wait_ge(y0_sb.sem, y0_sb.at(p3))
                    for g in range(G):
                        v.scalar_tensor_tensor(hop2[:, g, :], bank[3][1][:, g * F:(g + 1) * F], sum_inv[:, g:g + 1],
                                               y0[:, g, :], ALU.mult, ALU.add).then_inc(hop2_sb.sem, 1)

            all_steps(dve, step)

        @block.gpsimd
        def _(pool):
            gp = nc.gpsimd
            gp.memset(ident[:], 0.0).then_inc(ident_zero, 1)
            pool.wait_ge(ident_zero, 1)
            gp.affine_select(out=ident[:], in_=ident[:], compare_op=ALU.not_equal, fill=1.0, base=0,
                             pattern=[[-1, P]], channel_multiplier=1).then_inc(ident_made, 1)
            gp.memset(ones[:], 1.0).then_inc(consts_set, 1)
            gp.memset(neg_half[:], -0.5).then_inc(consts_set, 1)
            pool.wait_ge(consts_set, 2)
            pool.wait_ge(consts_in, CONSTS)

            def flat(a):
                return a[:].rearrange("p a b -> p (a b)")

            def root(n, p):
                pool.wait_ge(averaged[n].sem, averaged[n].at(p))
                if later(p):
                    pool.wait_ge(normed[n].sem, normed[n].at(p - 1))
                gp.tensor_tensor(rstd[n][:], var_eps[n][:], neg_half[:], ALU.pow).then_inc(rooted[n].sem, 1)
                if n != "lnh":
                    pool.wait_ge(rooted[n].sem, rooted[n].at(p))
                    gp.tensor_tensor(shift[n][:], neg_mean[n][:], rstd[n][:], ALU.mult).then_inc(shifted[n].sem, 1)

            def step(t, on):
                p0, p1, p2, p3, p4 = t, t - 1, t - 2, t - 3, t - 4
                if 2 in on:
                    root("ln1", p2)
                if 1 in on:
                    pool.wait_ge(normed["ln0"].sem, normed["ln0"].at(p1))
                    if later(p1):
                        pool.wait_ge(r1_based.sem, r1_based.at(p1 - 1))
                    gp.tensor_tensor(flat(xx), flat(x1), flat(hyp_b2_rows), ALU.add).then_inc(xx_half.sem, 1)
                    pool.wait_ge(xx_half.sem, xx_half.at(p1))
                    gp.tensor_tensor(flat(xx), flat(xx), flat(x1), ALU.add).then_inc(xx_made.sem, 1)
                if 0 in on:
                    pool.wait_ge(x_loaded.sem, x_loaded.at(p0))
                    if later(p0):
                        pool.wait_ge(summed["ln0"].sem, summed["ln0"].at(p0 - 1))
                    gp.tensor_tensor(flat(x_b3), flat(x_in), flat(b3_rows), ALU.add).then_inc(x_b3_made.sem, 1)
                if 1 in on:
                    root("lnh", p1)
                if 4 in on:
                    root("ln3", p4)
                if 3 in on:
                    pool.wait_ge(e_maxed.sem, e_maxed.at(p3))
                    pool.wait_ge(adj3_kept.sem, adj3_kept.at(p3))
                    if later(p3):
                        pool.wait_ge(hop2_ps.sem, hop2_ps.at(p3 - 1))
                    for g in range(G):
                        gp.tensor_tensor(alphaT[:, g, :], e_max[:, g, :], adjT3[:, g, :],
                                         ALU.mult).then_inc(alpha_made.sem, 1)
                    pool.wait_ge(y0_raw.sem, y0_raw.at(p3))
                    if later(p3):
                        pool.wait_ge(hop2_sb.sem, hop2_sb.at(p3 - 1))
                    gp.tensor_tensor(flat(y0), flat(y0_plain), flat(bk_sum), ALU.add).then_inc(y0_sb.sem, 1)
                if 2 in on:
                    root("ln2", p2)
                if 0 in on:
                    root("ln0", p0)

            all_steps(pool, step)

    return nc


_INS = ["x", "adj", "L0_gnn_W1", "L0_gnn_b1", "L0_gnn_W2", "L0_gnn_b2", "L0_gnn_W3", "L0_gnn_b3",
        "L1_gnn_W1", "L1_gnn_b1", "L1_gnn_gamma", "L1_gnn_beta", "L1_gnn_W2", "L1_gnn_b2",
        "L2_gnn_W_qk", "L2_gnn_W_v",
        "L3_gnn_Wv", "L3_gnn_bv", "L3_gnn_aw", "L3_gnn_ab", "L3_gnn_Wk", "L3_gnn_bk"]


def kernel(**inputs):
    import numpy as np
    import concourse.bacc as bacc
    from concourse.bass_utils import run_bass_kernel_spmd

    nc = bacc.Bacc("TRN2", target_bir_lowering=False, num_devices=1)
    arrays, args = {}, []
    for name in _INS:
        a = np.ascontiguousarray(inputs[name])
        arrays[f"in_{name}"] = a
        args.append(nc.dram_tensor(f"in_{name}", a.shape, mybir.dt.from_np(a.dtype), kind="ExternalInput").ap())
    args.append(nc.dram_tensor("out", inputs["x"].shape, F32, kind="ExternalOutput").ap())
    graph_block_kernel(nc, *args)
    return run_bass_kernel_spmd(nc, [arrays], core_ids=[0]).results[0]["out"]
```

```python
from contextlib import ExitStack

import concourse.bass as bass
from concourse import mybir

ALU = mybir.AluOpType
ACT = mybir.ActivationFunctionType
AX = mybir.AxisListType
F32 = mybir.dt.float32
F32R = mybir.dt.float32r

P = 128
EPS = 1e-5
TINY = 1.1754944e-38


class Signal:

    def __init__(self, sem, per_pair):
        self.sem, self.per = sem, per_pair

    def at(self, pair, k=None):
        return pair * self.per + (self.per if k is None else k)


def graph_block_kernel(
    nc, x, adj,
    gcn_w1, gcn_b1, gcn_w2, gcn_b2, gcn_w3, gcn_b3,
    hyp_w1, hyp_b1, hyp_gamma, hyp_beta, hyp_w2, hyp_b2,
    att_wqk, att_wv,
    dif_wv, dif_bv, dif_aw, dif_ab, dif_wk, dif_bk,
    out,
):
    B, N, F = x.shape
    G = 2
    PAIRS = B // G
    FC = F // P
    DH = hyp_w1.shape[0]
    HC = DH // P
    QK = att_wqk.shape[0]
    DA = QK // 2
    QKV = QK + F
    HOPS = dif_wk.shape[0]
    INV_SCALE = 1.0 / DA ** 0.5
    assert N == P and F == 2 * P and HC == 4 and HOPS == 3
    LAYERS = 4
    STAGES = LAYERS + 1

    x_pairs = x.rearrange("(s g) n f -> s n g f", g=G)
    adj_pairs = adj.rearrange("(s g) n m -> s n g m", g=G)
    out_pairs = out.rearrange("(s g) n f -> s n g f", g=G)

    with ExitStack() as ctx:
        def sb(name, shape, dtype=F32):
            return ctx.enter_context(nc.sbuf_tensor(name, shape, dtype))

        def halves(name, shape):
            return sb(name + "_hi", shape, F32R), sb(name + "_lo", shape, F32R)

        def sem(name):
            return ctx.enter_context(nc.semaphore(name))

        def signal(name, per_pair=1):
            return Signal(sem(name), per_pair)

        ident = sb("ident", [P, P])
        neg_half = sb("neg_half", [P, G])
        w1_raw = sb("w1_raw", [P, FC, F])
        w1 = halves("w1", [P, FC, F])
        w2_raw = sb("w2_raw", [P, FC, F])
        w2 = halves("w2", [P, FC, F])
        w3_raw = sb("w3_raw", [P, FC, F])
        w3 = halves("w3", [P, FC, F])
        gamma_rows, beta_rows, bv_rows, b1_rows, b2_rows, aw_rows = (
            slice(a, b) for a, b in ((0, HC), (HC, 2 * HC), (2 * HC, 2 * HC + FC), (2 * HC + FC, 2 * HC + 2 * FC),
                                     (2 * HC + 2 * FC, 2 * HC + 3 * FC), (2 * HC + 3 * FC, 2 * HC + 5 * FC)))
        VECS = 2 * HC + 5 * FC
        vec_rows = sb("vec_rows", [VECS, P])
        vec_cols = sb("vec_cols", [P, VECS])
        gamma_col, beta_col, bv_col, b1_col, b2_col = (
            vec_cols[:, rows] for rows in (gamma_rows, beta_rows, bv_rows, b1_rows, b2_rows))
        aw_cols = vec_cols[:, aw_rows].rearrange("p (h c) -> p h c", h=2)
        b3_rows = sb("b3_rows", [P, G, F])
        hyp_w1_nat = sb("hyp_w1_nat", [P, HC, F])
        hyp_w1T = halves("hyp_w1T", [P, FC, DH])
        hyp_b1_rows = sb("hyp_b1_rows", [P, DH])
        hyp_w2_nat = sb("hyp_w2_nat", [P, FC, DH])
        hyp_w2T = sb("hyp_w2T", [P, HC, F])
        hyp_w2g_raw = sb("hyp_w2g_raw", [P, HC, F])
        hyp_w2c_raw = sb("hyp_w2c_raw", [P, HC, F])
        hyp_w2c = halves("hyp_w2c", [P, HC, F])
        mean_rows = sb("mean_rows", [P, P])
        hyp_shift = sb("hyp_shift", [P, F])
        hyp_b2_rows = sb("hyp_b2_rows", [P, G, F])
        wqk_nat = sb("wqk_nat", [P, F])
        wv_nat = sb("wv_nat", [P, FC, F])
        w_qkv = halves("w_qkv", [P, FC, QKV])
        dif_wv_nat = sb("dif_wv_nat", [P, FC, F])
        dif_wvT = sb("dif_wvT", [P, FC, F])
        ab_col = sb("ab_col", [P, 1])
        wa_raw = sb("wa_raw", [P, FC, 2])
        s_const = sb("s_const", [P, 1])
        s_part = sb("s_part", [P, 2])
        w_hop_raw = sb("w_hop_raw", [P, FC, HOPS, F])
        w_hop01 = halves("w_hop01", [P, FC, 2 * F])
        w_s_hop2 = halves("w_s_hop2", [P, FC, 2 + F])
        bk_rows = sb("bk_rows", [P, HOPS, F])
        bk_tmp = sb("bk_tmp", [P, F])
        bk_sum = sb("bk_sum", [P, G, F])

        x_in = sb("x_in", [P, G, F])
        adj_in = sb("adj_in", [P, G, N])
        adjT0 = sb("adjT0", [P, G, N])
        x_b3 = sb("x_b3", [P, G, F])
        axT = halves("axT", [P, FC, G, N])
        h1T_raw = sb("h1T_raw", [P, FC, G, N])
        h1T = halves("h1T", [P, FC, G, N])
        s2 = sb("s2", [P, G, F])
        h2T_raw = sb("h2T_raw", [P, FC, G, N])
        h2T = halves("h2T", [P, FC, G, N])
        s3 = sb("s3", [P, G, F])
        r0 = sb("r0", [P, G, F])
        x1 = sb("x1", [P, G, F])
        incT = sb("incT", [P, G, N])
        incT_w = sb("incT_w", [P, G, N + 2])
        edge_size = sb("edge_size", [P, G])
        edge_size1 = sb("edge_size1", [P, G])
        edge_inv = sb("edge_inv", [P, G])
        adjT1 = sb("adjT1", [P, G, N])
        kdeg = sb("kdeg", [P, G, N + 2])
        kmat = kdeg[:, :, 0:N]
        deg = kdeg[:, :, N:N + 2]
        deg_pos = sb("deg_pos", [P, G])
        deg_safe = sb("deg_safe", [P, G])
        deg_rec = sb("deg_rec", [P, G])
        deg_inv = sb("deg_inv", [P, G])
        row_sum = sb("row_sum", [P, G])
        kxT = halves("kxT", [P, FC, G, N])
        h_pre = sb("h_pre", [P, G, DH])
        h_act = sb("h_act", [P, G, DH])
        kmat_r = sb("kmat_r", [P, G, N])
        kzT = halves("kzT", [P, G, HC, N])
        xx = sb("xx", [P, G, F])
        r1_base = sb("r1_base", [P, G, F])
        r1 = sb("r1", [P, G, F])
        x2 = sb("x2", [P, G, F])
        adjT2 = sb("adjT2", [P, G, N])
        x2T = halves("x2T", [P, FC, G, N])
        qkv = sb("qkv", [P, G, QKV])
        qak = sb("qak", [P, G, DA])
        score = sb("score", [P, G])
        neg_max = sb("neg_max", [G, 1])
        prob_e = sb("prob_e", [G, N])
        prob_sum = sb("prob_sum", [G, 1])
        prob_inv = sb("prob_inv", [G, 1])
        prob_row = sb("prob_row", [G, N])
        prob = sb("prob", [P, G])
        r2 = sb("r2", [P, G, F])
        x3 = sb("x3", [P, G, F])
        adjT3 = sb("adjT3", [P, G, N])
        x3T = halves("x3T", [P, FC, G, N])
        s_col = sb("s_col", [P, G])
        s_col02 = sb("s_col02", [P, G])
        e_pos = sb("e_pos", [P, G, N])
        e_neg = sb("e_neg", [P, G, N])
        e_max = sb("e_max", [P, G, N])
        alphaT = sb("alphaT", [P, G, N])
        sum_eps = sb("sum_eps", [P, G])
        sum_inv = sb("sum_inv", [P, G])
        s_y2 = sb("s_y2", [P, G, 2 + F + 1])
        y01 = sb("y01", [P, G, 2 * F])
        y0 = sb("y0", [P, G, F])
        hop1 = sb("hop1", [P, G, F])
        hop2 = sb("hop2", [P, G, F])
        x3_kept = sb("x3_kept", [P, G, F])
        r3 = sb("r3", [P, G, F])
        y_out = sb("y_out", [P, G, F])

        NORMS = ("ln0", "lnh", "ln1", "ln2", "ln3")
        stats = {n: sb(n + "_stats", [P, G, 6]) for n in NORMS}
        mean_gap = {n: sb(n + "_mean_gap", [P, G]) for n in NORMS}
        gap_square = {n: sb(n + "_gap_square", [P, G]) for n in NORMS}
        square_sum = {n: sb(n + "_square_sum", [P, G]) for n in NORMS}
        neg_mean = {n: sb(n + "_neg_mean", [P, G]) for n in NORMS if n != "lnh"}
        shift = {n: sb(n + "_shift", [P, G]) for n in NORMS if n != "lnh"}
        var_eps = {n: sb(n + "_var_eps", [P, G]) for n in NORMS}
        rstd = {n: sb(n + "_rstd", [P, G]) for n in NORMS}

        bank = [[ctx.enter_context(nc.psum_tensor(f"layer{l}_{b}", [P, 512], F32)) for b in range(2)]
                for l in range(LAYERS)]

        turned_in, consts_in, ident_zero, ident_made, consts_set = map(
            sem, ("turned_in", "consts_in", "ident_zero", "ident_made", "consts_set"))
        weights_turned, weights_kept, gamma_in, w2_averaged, mean_off, split_hi, split_lo, shifts_made, bias_summed = map(
            sem, ("weights_turned", "weights_kept", "gamma_in", "w2_averaged", "mean_off", "split_hi", "split_lo",
                  "shifts_made", "bias_summed"))
        setup_done = sem("setup_done")
        x_loaded, adj_loaded, y_stored = signal("x_loaded", 16), signal("adj_loaded", 16), signal("y_stored", 16)
        adjT_ps, ax_ps, h1_ps, s2_ps, as2_ps, s3_ps, gcn_ps = (
            signal(n) for n in ("adjT_ps", "ax_ps", "h1_ps", "s2_ps", "as2_ps", "s3_ps", "gcn_ps"))
        k_ps, kx_ps, hyp2_ps = (signal(n) for n in ("k_ps", "kx_ps", "hyp2_ps"))
        hyp1_ps, kz_ps = signal("hyp1_ps", 2), signal("kz_ps", 2)
        x2T_ps, ak_ps, score_ps, prob_ps = (signal(n) for n in ("x2T_ps", "ak_ps", "score_ps", "prob_ps"))
        qkv_ps = signal("qkv_ps", 2)
        x3T_ps, s_row_ps, hop2_ps = (signal(n) for n in ("x3T_ps", "s_row_ps", "hop2_ps"))
        s_y2_ps, y01_ps, hop1_ps = signal("s_y2_ps", 2), signal("y01_ps", 2), signal("hop1_ps", 2)
        h1_hi, h1_lo, h2_hi, h2_lo = (signal(n) for n in ("h1_hi", "h1_lo", "h2_hi", "h2_lo"))
        adjT_sb, ax_hi, s2_sb, s3_sb, k_sb, kx_hi, x2T_hi, x3T_hi = (
            signal(n) for n in (
                "adjT_sb", "ax_hi", "s2_sb", "s3_sb", "k_sb", "kx_hi", "x2T_hi", "x3T_hi"))
        h1_sb, h2_sb, kz_hi, qkv_sb, s_y2_sb, y01_sb, relu_sb = (
            signal(n, 2) for n in ("h1_sb", "h2_sb", "kz_hi", "qkv_sb", "s_y2_sb", "y01_sb", "relu_sb"))
        edge_exp, prob_exp = signal("edge_exp", 4), signal("prob_exp")
        ax_lo, kx_lo, x2T_lo, x3T_lo, kz_lo = (
            signal("ax_lo"), signal("kx_lo"), signal("x2T_lo"), signal("x3T_lo"), signal("kz_lo", 2))
        inc_made = signal("inc_made", 2)
        size_floor, size_inv, deg_rhs_set = signal("size_floor"), signal("size_inv"), signal("deg_rhs_set", 2)
        incw_made = signal("incw_made", 2)
        deg_prep, deg_recip, deg_done = signal("deg_prep", 2), signal("deg_recip"), signal("deg_done", 2)
        hyp1_pre = signal("hyp1_pre", 2)
        r1_based = signal("r1_based", 2)
        scored, max_found, sum_inverted, prob_normed, prob_sb = (
            signal("scored", 2), signal("max_found"), signal("sum_inverted"), signal("prob_normed"), signal("prob_sb"))
        s_sb, s02_sb, e_maxed, y0_sb, rsum_eps, rsum_inv, hop1_sb, hop2_sb = (
            signal("s_sb"), signal("s02_sb"), signal("e_maxed"), signal("y0_sb"),
            signal("rsum_eps", 2), signal("rsum_inv"), signal("hop1_sb", 2), signal("hop2_sb", 2))
        summed = {n: signal(n + "_summed", 1 if n in ("ln0", "ln3") else 2) for n in NORMS if n != "lnh"}
        stated = {n: signal(n + "_stated", 2) for n in NORMS}
        gap_taken = {n: signal(n + "_gap_taken", 2) for n in NORMS}
        gap_used = {n: signal(n + "_gap_used", 1 if n == "lnh" else 2) for n in NORMS}
        averaged = {n: signal(n + "_averaged") for n in NORMS}
        normed = {n: signal(n + "_normed", 2) for n in NORMS}
        rooted = {n: signal(n + "_rooted") for n in NORMS}
        shifted = {n: signal(n + "_shifted") for n in NORMS if n != "lnh"}
        x_b3_made, xx_half, xx_made = (signal(n) for n in ("x_b3_made", "xx_half", "xx_made"))
        alpha_made = signal("alpha_made", 2)
        adj1_kept, adj2_kept, adj3_kept, x3_copied = (
            signal(n, 16) for n in ("adj1_kept", "adj2_kept", "adj3_kept", "x3_copied"))

        def later(pair):
            return not (isinstance(pair, int) and pair == 0)

        def all_steps(eng, step):
            for t in range(STAGES):
                step(t, range(t + 1))
            with eng.Fori(STAGES, PAIRS) as t:
                step(t, range(STAGES))
            for t in range(PAIRS, PAIRS + STAGES - 1):
                step(t, range(t - PAIRS + 1, STAGES))

        turn_dmas = [(dst[:], src.rearrange("(c p) n -> p c n", p=P)) for dst, src in (
            (hyp_w2_nat, hyp_w2), (dif_wv_nat, dif_wv), (hyp_w1_nat, hyp_w1), (wv_nat, att_wv))]
        turn_dmas.append((wqk_nat[:], att_wqk))
        for rows, src in ((gamma_rows, hyp_gamma), (beta_rows, hyp_beta), (bv_rows, dif_bv), (b1_rows, gcn_b1),
                          (b2_rows, gcn_b2), (aw_rows, dif_aw.rearrange("n a -> (n a)"))):
            turn_dmas.append((vec_rows[rows, :], src.rearrange("(c p) -> c p", p=P)))
        const_dmas = []
        for dst, src in ((w1_raw, gcn_w1), (w2_raw, gcn_w2), (w3_raw, gcn_w3)):
            const_dmas.append((dst[:], src.rearrange("(c p) n -> p c n", p=P)))
        for k in range(HOPS):
            const_dmas.append((w_hop_raw[:, :, k, :], dif_wk[k].rearrange("(c p) n -> p c n", p=P)))
        const_dmas += [(bk_rows[:].rearrange("p k n -> p (k n)"), dif_bk.rearrange("k n -> (k n)").partition_broadcast(P)),
                       (hyp_b1_rows[:], hyp_b1.partition_broadcast(P)), (ab_col[:], dif_ab.partition_broadcast(P))]
        for g in range(G):
            const_dmas.append((b3_rows[:, g, :], gcn_b3.partition_broadcast(P)))
            const_dmas.append((hyp_b2_rows[:, g, :], hyp_b2.partition_broadcast(P)))
        TURNED, CONSTS = 16 * len(turn_dmas), 16 * len(const_dmas)
        SETUP = 7
        KEPT = 4

        def rows(pair, c):
            return pair[0][:, c, :], pair[1][:, c, :]

        def whole(a):
            return a[:].rearrange("p a b -> p (a b)")

        weight_halves = {}
        for c in range(FC):
            weight_halves[f"hyp_w1T_{c}"] = rows(hyp_w1T, c), bank[0][c][:]
            weight_halves[f"w_qkv_{c}"] = rows(w_qkv, c), bank[2][c][:, 0:QKV]
            weight_halves[f"w_hop01_{c}"] = rows(w_hop01, c), w_hop_raw[:, c, 0:2, :].rearrange("p k n -> p (k n)")
        for name, pair, raw in (("w1", w1, w1_raw), ("w2", w2, w2_raw), ("w3", w3, w3_raw),
                                ("hyp_w2c", hyp_w2c, hyp_w2c_raw)):
            weight_halves[name] = (whole(pair[0]), whole(pair[1])), whole(raw)
        weight_halves["w_hop2"] = (w_s_hop2[0][:, :, 2:2 + F], w_s_hop2[1][:, :, 2:2 + F]), w_hop_raw[:, :, 2, :]
        weight_halves["w_s"] = (w_s_hop2[0][:, :, 0:2], w_s_hop2[1][:, :, 0:2]), wa_raw[:]
        TURNED_WEIGHTS = [f"{w}_{c}" for w in ("hyp_w1T", "w_qkv") for c in range(FC)]
        LOADED_WEIGHTS = ["w1", "w2", "w3", "w_hop01_0", "w_hop01_1", "w_hop2"]
        MADE_WEIGHTS = ["hyp_w2c", "w_s"]
        SPLIT_ORDER = TURNED_WEIGHTS + LOADED_WEIGHTS + MADE_WEIGHTS

        block = ctx.enter_context(nc.Block())

        @block.sync
        def _(sp):
            for dst, src in turn_dmas:
                sp.dma_start(dst, src).then_inc(turned_in, 16)
            for dst, src in const_dmas:
                sp.dma_start(dst, src).then_inc(consts_in, 16)

            def load_adj(t):
                if later(t):
                    sp.wait_ge(adjT_ps.sem, adjT_ps.at(t - 1))
                sp.dma_start(adj_in[:], adj_pairs[t]).then_inc(adj_loaded.sem, 16)

            def load_x(t):
                if later(t):
                    sp.wait_ge(ax_ps.sem, ax_ps.at(t - 1))
                    sp.wait_ge(x_b3_made.sem, x_b3_made.at(t - 1))
                sp.dma_start(x_in[:], x_pairs[t]).then_inc(x_loaded.sem, 16)

            def step(t, on):
                p0, p1, p2, p3, p4 = t, t - 1, t - 2, t - 3, t - 4
                if 3 in on:
                    if later(p3):
                        sp.wait_ge(summed["ln3"].sem, summed["ln3"].at(p3 - 1))
                    sp.wait_ge(normed["ln2"].sem, normed["ln2"].at(p3))
                    sp.dma_start(x3_kept[:], x3[:]).then_inc(x3_copied.sem, 16)
                if 2 in on:
                    sp.wait_ge(ak_ps.sem, ak_ps.at(p2))
                    if later(p2):
                        sp.wait_ge(alpha_made.sem, alpha_made.at(p2 - 1))
                    sp.dma_start(adjT3[:], adjT2[:]).then_inc(adj3_kept.sem, 16)
                if 4 in on:
                    sp.wait_ge(normed["ln3"].sem, normed["ln3"].at(p4))
                    sp.dma_start(out_pairs[p4], y_out[:]).then_inc(y_stored.sem, 16)
                if 0 in on and not (isinstance(p0, int) and p0 == PAIRS - 1):
                    load_adj(p0 + 1)
                    load_x(p0 + 1)
                if 1 in on:
                    if later(p1):
                        sp.wait_ge(adj3_kept.sem, adj3_kept.at(p1 - 1))
                    sp.wait_ge(adj1_kept.sem, adj1_kept.at(p1))
                    sp.dma_start(adjT2[:], adjT1[:]).then_inc(adj2_kept.sem, 16)
                if 0 in on:
                    sp.wait_ge(gcn_ps.sem, gcn_ps.at(p0))
                    sp.wait_ge(deg_rhs_set.sem, deg_rhs_set.at(p0))
                    if later(p0):
                        sp.wait_ge(adj2_kept.sem, adj2_kept.at(p0 - 1))
                    sp.dma_start(adjT1[:], adjT0[:]).then_inc(adj1_kept.sem, 16)

            load_adj(0)
            load_x(0)
            for t in range(STAGES):
                step(t, range(t + 1))
            with sp.Fori(STAGES, PAIRS - 1) as t:
                step(t, range(STAGES))
            for t in range(PAIRS - 1, PAIRS + STAGES - 1):
                step(t, range(max(0, t - PAIRS + 1), STAGES))
            sp.wait_ge(y_stored.sem, y_stored.at(PAIRS - 1))

        @block.tensor
        def _(pe):
            mm, turn = nc.tensor.matmul, nc.tensor.transpose
            everything = bank[0] + bank[1] + bank[2] + bank[3]

            pe.wait_ge(turned_in, TURNED)
            pe.wait_ge(ident_made, 1)
            for c in range(FC):
                for h in range(HC):
                    turn(everything[c][:, h * P:(h + 1) * P], hyp_w1_nat[:, h, c * P:(c + 1) * P], ident[:])
            for h in range(HC):
                for o in range(FC):
                    at = (h % 2) * F + o * P
                    turn(everything[2 + h // 2][:, at:at + P], hyp_w2_nat[:, o, h * P:(h + 1) * P], ident[:])
            for c in range(FC):
                turn(everything[4 + c][:, 0:QK], wqk_nat[:, c * P:(c + 1) * P], ident[:])
                for o in range(FC):
                    turn(everything[4 + c][:, QK + o * P:QK + (o + 1) * P], wv_nat[:, o, c * P:(c + 1) * P], ident[:])
            for o in range(FC):
                for c in range(FC):
                    turn(everything[6][:, o * F + c * P:o * F + (c + 1) * P],
                         dif_wv_nat[:, c, o * P:(o + 1) * P], ident[:])
            turn(everything[7][:, 0:VECS], vec_rows[:], ident[0:VECS, 0:VECS]).then_inc(weights_turned, 1)
            pe.wait_ge(weights_kept, KEPT)
            for h in range(HC):
                mm(everything[7][:, 0:F], beta_col[:, h:h + 1].to_broadcast([P, P]), hyp_w2T[:, h, :],
                   start=(h == 0), stop=(h == HC - 1))
            for c in range(FC):
                for o in range(FC):
                    mm(everything[7][:, F + 2 * c:F + 2 * c + 2], dif_wvT[:, o, c * P:(c + 1) * P], aw_cols[:, :, o],
                       start=(o == 0), stop=(o == FC - 1))
            for o in range(FC):
                last = mm(everything[7][:, F + 8:F + 10], bv_col[:, o:o + 1].to_broadcast([P, P]), aw_cols[:, :, o],
                          start=(o == 0), stop=(o == FC - 1))
            last.then_inc(shifts_made, 1)
            pe.wait_ge(consts_set, 3)
            pe.wait_ge(gamma_in, HC)
            for h in range(HC):
                last = mm(everything[6][:, 0:F], mean_rows[:], hyp_w2g_raw[:, h, :],
                          start=(h == 0), stop=(h == HC - 1))
            last.then_inc(w2_averaged, 1)
            pe.wait_ge(setup_done, SETUP)

            def turn_x(dst, src):
                for c in range(FC):
                    for g in range(G):
                        at = (c * G + g) * N
                        last = turn(dst[:, at:at + N], src[:, g, c * P:(c + 1) * P], ident[:])
                return last

            def nodes_mix(dst, src, mix):
                for c in range(FC):
                    for g in range(G):
                        at = (c * G + g) * N
                        last = mm(dst[:, at:at + N], src[:, g, c * P:(c + 1) * P], mix[:, g, :], start=True, stop=True)
                return last

            def mm3(dst, lhsT, rhs, start, stop):
                mm(dst, lhsT[0], rhs[0], start=start, stop=False)
                mm(dst, lhsT[0], rhs[1], start=False, stop=False)
                return mm(dst, lhsT[1], rhs[0], start=False, stop=stop)

            def part(pair, *at):
                return pair[0][at], pair[1][at]

            ALL = slice(None)

            def weigh(dst, srcT, w):
                for g in range(G):
                    for c in range(FC):
                        last = mm3(dst[:, g * F:(g + 1) * F], part(srcT, ALL, c, g, ALL), part(w, ALL, c, ALL),
                                   start=(c == 0), stop=(c == FC - 1))
                return last

            def graph_mix(g, p):
                pe.wait_ge(normed["lnh"].sem, normed["lnh"].at(p, g + 1))
                for h in range(HC):
                    last = mm(bank[1][1 - g][:, h * N:(h + 1) * N], h_act[:, g, h * P:(h + 1) * P], kmat_r[:, g, :],
                              start=True, stop=True)
                last.then_inc(kz_ps.sem, 1)

            def hyper_widen(g):
                for c in range(FC):
                    last = mm3(bank[1][1 - g][:, 0:DH], part(kxT, ALL, c, g, ALL), part(hyp_w1T, ALL, c, ALL),
                               start=(c == 0), stop=(c == FC - 1))
                return last

            def hyper_narrow(g):
                for h in range(HC):
                    last = mm3(bank[1][0][:, g * F:(g + 1) * F], part(kzT, ALL, g, h, ALL), part(hyp_w2c, ALL, h, ALL),
                               start=(h == 0), stop=(h == HC - 1))
                return last

            def attend(g):
                for c in range(FC):
                    last = mm3(bank[2][1 - g][:, 0:QKV], part(x2T, ALL, c, g, ALL), part(w_qkv, ALL, c, ALL),
                               start=(c == 0), stop=(c == FC - 1))
                return last

            def score_and_last_hop(g):
                for c in range(FC):
                    last = mm3(bank[3][g][:, 0:2 + F], part(x3T, ALL, c, g, ALL), part(w_s_hop2, ALL, c, ALL),
                               start=(c == 0), stop=(c == FC - 1))
                return last

            def first_hops(g):
                for c in range(FC):
                    last = mm3(bank[3][1 - g][:], part(x3T, ALL, c, g, ALL), part(w_hop01, ALL, c, ALL),
                               start=(c == 0), stop=(c == FC - 1))
                return last

            def step(t, on):
                p0, p1, p2, p3, p4 = t, t - 1, t - 2, t - 3, t - 4
                if 0 in on:
                    pe.wait_ge(adj_loaded.sem, adj_loaded.at(p0))
                    if later(p0):
                        pe.wait_ge(summed["ln0"].sem, summed["ln0"].at(p0 - 1))
                    for g in range(G):
                        last = turn(bank[0][0][:, g * N:(g + 1) * N], adj_in[:, g, :], ident[:])
                    last.then_inc(adjT_ps.sem, 1)
                if 3 in on:
                    pe.wait_ge(normed["ln2"].sem, normed["ln2"].at(p3))
                    if later(p3):
                        pe.wait_ge(hop1_sb.sem, hop1_sb.at(p3 - 1))
                    turn_x(bank[3][0], x3).then_inc(x3T_ps.sem, 1)
                if 0 in on:
                    pe.wait_ge(adjT_sb.sem, adjT_sb.at(p0))
                    pe.wait_ge(x_loaded.sem, x_loaded.at(p0))
                    if later(p0):
                        pe.wait_ge(s3_sb.sem, s3_sb.at(p0 - 1))
                    nodes_mix(bank[0][1], x_in, adjT0).then_inc(ax_ps.sem, 1)
                if 1 in on:
                    pe.wait_ge(k_sb.sem, k_sb.at(p1))
                    pe.wait_ge(normed["ln0"].sem, normed["ln0"].at(p1))
                    if later(p1):
                        pe.wait_ge(summed["ln1"].sem, summed["ln1"].at(p1 - 1))
                    nodes_mix(bank[1][0], x1, kmat).then_inc(kx_ps.sem, 1)
                if 3 in on:
                    pe.wait_ge(x3T_lo.sem, x3T_lo.at(p3))
                    score_and_last_hop(0).then_inc(s_y2_ps.sem, 1)
                    if later(p3):
                        pe.wait_ge(hop2_sb.sem, hop2_sb.at(p3 - 1))
                    score_and_last_hop(1).then_inc(s_y2_ps.sem, 1)
                if 0 in on:
                    pe.wait_ge(ax_lo.sem, ax_lo.at(p0))
                    for h in range(FC):
                        for c in range(FC):
                            last = mm3(bank[0][0][:, h * G * N:(h + 1) * G * N], part(w1, ALL, c, slice(h * P, (h + 1) * P)),
                                       part(axT, ALL, c, ALL, ALL), start=(c == 0), stop=(c == FC - 1))
                    last.then_inc(h1_ps.sem, 1)
                if 2 in on:
                    pe.wait_ge(normed["ln1"].sem, normed["ln1"].at(p2))
                    if later(p2):
                        pe.wait_ge(prob_sb.sem, prob_sb.at(p2 - 1))
                    turn_x(bank[2][0], x2).then_inc(x2T_ps.sem, 1)
                if 1 in on:
                    pe.wait_ge(kx_lo.sem, kx_lo.at(p1))
                    hyper_widen(0).then_inc(hyp1_ps.sem, 1)
                    hyper_widen(1).then_inc(hyp1_ps.sem, 1)
                if 2 in on:
                    pe.wait_ge(x2T_lo.sem, x2T_lo.at(p2))
                    attend(0).then_inc(qkv_ps.sem, 1)
                if 0 in on:
                    pe.wait_ge(h1_lo.sem, h1_lo.at(p0))
                    weigh(bank[0][1], h1T, w2).then_inc(s2_ps.sem, 1)
                if 2 in on:
                    attend(1).then_inc(qkv_ps.sem, 1)
                if 3 in on:
                    pe.wait_ge(s_y2_sb.sem, s_y2_sb.at(p3))
                    for g in range(G):
                        last = turn(bank[3][0][:, g * N:(g + 1) * N], s_y2[:, g, 1:2].to_broadcast([P, P]), ident[:])
                    last.then_inc(s_row_ps.sem, 1)
                if 0 in on:
                    pe.wait_ge(s2_sb.sem, s2_sb.at(p0))
                    nodes_mix(bank[0][0], s2, adjT0).then_inc(as2_ps.sem, 1)
                if 2 in on:
                    pe.wait_ge(qkv_sb.sem, qkv_sb.at(p2))
                    pe.wait_ge(adj2_kept.sem, adj2_kept.at(p2))
                    for g in range(G):
                        last = mm(bank[2][1][:, g * DA:(g + 1) * DA], adjT2[:, g, :], qkv[:, g, DA:2 * DA],
                                  start=True, stop=True)
                    last.then_inc(ak_ps.sem, 1)
                if 3 in on:
                    first_hops(0).then_inc(y01_ps.sem, 1)
                if 2 in on:
                    pe.wait_ge(scored.sem, scored.at(p2))
                    mm(bank[2][0][0:G, 0:N], score[:], ident[:], start=True, stop=True).then_inc(score_ps.sem, 1)
                if 1 in on:
                    graph_mix(0, p1)
                if 3 in on:
                    pe.wait_ge(edge_exp.sem, edge_exp.at(p3))
                    first_hops(1).then_inc(y01_ps.sem, 1)
                if 2 in on:
                    pe.wait_ge(prob_normed.sem, prob_normed.at(p2))
                    mm(bank[2][0][:, 0:G], prob_row[:], ident[0:G, 0:G], start=True, stop=True).then_inc(prob_ps.sem, 1)
                if 0 in on:
                    pe.wait_ge(h2_lo.sem, h2_lo.at(p0))
                    weigh(bank[0][1], h2T, w3).then_inc(s3_ps.sem, 1)
                if 1 in on:
                    graph_mix(1, p1)
                if 0 in on:
                    pe.wait_ge(s3_sb.sem, s3_sb.at(p0))
                    for g in range(G):
                        last = mm(bank[0][0][:, g * F:(g + 1) * F], adjT0[:, g, :], s3[:, g, :], start=True, stop=True)
                    last.then_inc(gcn_ps.sem, 1)
                if 3 in on:
                    for g in range(G):
                        pe.wait_ge(y01_sb.sem, y01_sb.at(p3, 2 - g))
                        pe.wait_ge(alpha_made.sem, alpha_made.at(p3, g + 1))
                        mm(bank[3][g][:, 0:F + 1], alphaT[:, g, :], s_y2[:, g, 2:2 + F + 1],
                           start=True, stop=True).then_inc(hop1_ps.sem, 1)
                if 1 in on:
                    pe.wait_ge(kz_lo.sem, kz_lo.at(p1))
                    hyper_narrow(0)
                    hyper_narrow(1).then_inc(hyp2_ps.sem, 1)
                if 0 in on:
                    pe.wait_ge(incw_made.sem, incw_made.at(p0))
                    pe.wait_ge(deg_rhs_set.sem, deg_rhs_set.at(p0))
                    if later(p0):
                        pe.wait_ge(kz_lo.sem, kz_lo.at(p0 - 1, 1))
                    for g in range(G):
                        last = mm(bank[1][1][:, g * (N + 2):(g + 1) * (N + 2)], incT[:, g, :], incT_w[:, g, :],
                                  start=True, stop=True)
                    last.then_inc(k_ps.sem, 1)
                if 3 in on:
                    pe.wait_ge(hop1_sb.sem, hop1_sb.at(p3))
                    for g in range(G):
                        last = mm(bank[3][1][:, g * F:(g + 1) * F], alphaT[:, g, :], hop1[:, g, :],
                                  start=True, stop=True)
                    last.then_inc(hop2_ps.sem, 1)

            all_steps(pe, step)

        @block.scalar
        def _(act):
            def copy(dst, src):
                return nc.scalar.activation(dst, src, ACT.Copy)

            def flat(a):
                return a[:].rearrange("p a b c -> p (a b c)") if len(a.shape) == 4 else a[:].rearrange("p a b -> p (a b)")

            def normalise(n, p, dst, src):
                act.wait_ge(shifted[n].sem, shifted[n].at(p))
                for g in range(G):
                    nc.scalar.activation(dst[:, g, :], src[:, g, :], ACT.Identity, bias=shift[n][:, g:g + 1],
                                         scale=rstd[n][:, g:g + 1]).then_inc(normed[n].sem, 1)

            def rectify(g, p):
                act.wait_ge(hyp1_pre.sem, hyp1_pre.at(p, g + 1))
                if later(p):
                    act.wait_ge(kz_ps.sem, kz_ps.at(p - 1, g + 1))
                nc.scalar.activation(h_act[:, g, :], h_pre[:, g, :], ACT.Relu).then_inc(relu_sb.sem, 1)

            def keep_hops(g, p):
                act.wait_ge(y01_ps.sem, y01_ps.at(p, g + 1))
                copy(y01[:, g, :], bank[3][1 - g][:]).then_inc(y01_sb.sem, 1)

            def keep_qkv(g, p):
                act.wait_ge(qkv_ps.sem, qkv_ps.at(p, g + 1))
                copy(qkv[:, g, :], bank[2][1 - g][:, 0:QKV]).then_inc(qkv_sb.sem, 1)

            def keep_mixed(g, p):
                act.wait_ge(kz_ps.sem, kz_ps.at(p, g + 1))
                copy(kzT[0][:, g, :, :].rearrange("p h n -> p (h n)"), bank[1][1 - g][:]).then_inc(kz_hi.sem, 1)

            def step(t, on):
                p0, p1, p2, p3, p4 = t, t - 1, t - 2, t - 3, t - 4
                if 0 in on:
                    act.wait_ge(adjT_ps.sem, adjT_ps.at(p0))
                    if later(p0):
                        act.wait_ge(adj1_kept.sem, adj1_kept.at(p0 - 1))
                    copy(flat(adjT0), bank[0][0][:, 0:G * N]).then_inc(adjT_sb.sem, 1)
                if 1 in on:
                    act.wait_ge(k_ps.sem, k_ps.at(p1))
                    if later(p1):
                        act.wait_ge(deg_done.sem, deg_done.at(p1 - 1))
                    copy(flat(kdeg), bank[1][1][:, 0:G * (N + 2)]).then_inc(k_sb.sem, 1)
                if 3 in on:
                    act.wait_ge(x3T_ps.sem, x3T_ps.at(p3))
                    copy(flat(x3T[0]), bank[3][0][:]).then_inc(x3T_hi.sem, 1)
                if 0 in on:
                    act.wait_ge(ax_ps.sem, ax_ps.at(p0))
                    copy(flat(axT[0]), bank[0][1][:]).then_inc(ax_hi.sem, 1)
                if 1 in on:
                    act.wait_ge(kx_ps.sem, kx_ps.at(p1))
                    copy(flat(kxT[0]), bank[1][0][:]).then_inc(kx_hi.sem, 1)
                if 2 in on:
                    normalise("ln1", p2, x2, r1)
                if 3 in on:
                    for g in range(G):
                        act.wait_ge(s_y2_ps.sem, s_y2_ps.at(p3, g + 1))
                        copy(s_y2[:, g, 0:2 + F], bank[3][g][:, 0:2 + F]).then_inc(s_y2_sb.sem, 1)
                if 0 in on:
                    act.wait_ge(h1_ps.sem, h1_ps.at(p0))
                    for c in range(FC):
                        nc.scalar.activation(h1T_raw[:, c, :, :], bank[0][0][:, c * G * N:(c + 1) * G * N], ACT.Relu,
                                             bias=b1_col[:, c:c + 1]).then_inc(h1_sb.sem, 1)
                if 2 in on:
                    act.wait_ge(x2T_ps.sem, x2T_ps.at(p2))
                    copy(flat(x2T[0]), bank[2][0][:]).then_inc(x2T_hi.sem, 1)
                if 0 in on:
                    act.wait_ge(h1_sb.sem, h1_sb.at(p0))
                    copy(flat(h1T[0]), flat(h1T_raw)).then_inc(h1_hi.sem, 1)
                if 1 in on:
                    rectify(0, p1)
                    rectify(1, p1)
                if 0 in on:
                    act.wait_ge(s2_ps.sem, s2_ps.at(p0))
                    copy(flat(s2), bank[0][1][:]).then_inc(s2_sb.sem, 1)
                if 2 in on:
                    if later(p2):
                        act.wait_ge(summed["ln2"].sem, summed["ln2"].at(p2 - 1))
                    keep_qkv(0, p2)
                    keep_qkv(1, p2)
                if 3 in on:
                    act.wait_ge(s_row_ps.sem, s_row_ps.at(p3))
                    act.wait_ge(s02_sb.sem, s02_sb.at(p3))
                    if later(p3):
                        act.wait_ge(e_maxed.sem, e_maxed.at(p3 - 1))
                    for g in range(G):
                        row = bank[3][0][:, g * N:(g + 1) * N]
                        nc.scalar.activation(e_pos[:, g, :], row, ACT.Exp,
                                             bias=s_col[:, g:g + 1]).then_inc(edge_exp.sem, 1)
                        nc.scalar.activation(e_neg[:, g, :], row, ACT.Exp, scale=0.2,
                                             bias=s_col02[:, g:g + 1]).then_inc(edge_exp.sem, 1)
                if 0 in on:
                    act.wait_ge(as2_ps.sem, as2_ps.at(p0))
                    for c in range(FC):
                        nc.scalar.activation(h2T_raw[:, c, :, :], bank[0][0][:, c * G * N:(c + 1) * G * N], ACT.Relu,
                                             bias=b2_col[:, c:c + 1]).then_inc(h2_sb.sem, 1)
                    act.wait_ge(h2_sb.sem, h2_sb.at(p0))
                    copy(flat(h2T[0]), flat(h2T_raw)).then_inc(h2_hi.sem, 1)
                if 3 in on:
                    if later(p3):
                        act.wait_ge(y0_sb.sem, y0_sb.at(p3 - 1))
                    keep_hops(0, p3)
                if 2 in on:
                    act.wait_ge(max_found.sem, max_found.at(p2))
                    if later(p2):
                        act.wait_ge(prob_normed.sem, prob_normed.at(p2 - 1))
                    nc.scalar.activation(prob_e[:], bank[2][0][0:G, 0:N], ACT.Exp, bias=neg_max[:],
                                         accum_out=prob_sum[:]).then_inc(prob_exp.sem, 1)
                if 1 in on:
                    keep_mixed(0, p1)
                if 4 in on:
                    if later(p4):
                        act.wait_ge(y_stored.sem, y_stored.at(p4 - 1))
                    normalise("ln3", p4, y_out, r3)
                if 3 in on:
                    keep_hops(1, p3)
                if 0 in on:
                    act.wait_ge(s3_ps.sem, s3_ps.at(p0))
                    copy(flat(s3), bank[0][1][:]).then_inc(s3_sb.sem, 1)
                if 1 in on:
                    keep_mixed(1, p1)
                if 2 in on:
                    if later(p2):
                        act.wait_ge(x3_copied.sem, x3_copied.at(p2 - 1))
                    normalise("ln2", p2, x3, r2)
                if 0 in on:
                    normalise("ln0", p0, x1, r0)

            for names, ready, value in ((TURNED_WEIGHTS, weights_turned, 1), (LOADED_WEIGHTS, consts_in, CONSTS),
                                        (MADE_WEIGHTS, mean_off, HC)):
                act.wait_ge(ready, value)
                if names is MADE_WEIGHTS:
                    act.wait_ge(setup_done, 5)
                for name in names:
                    (hi, lo), src = weight_halves[name]
                    copy(hi, src).then_inc(split_hi, 1)
            all_steps(act, step)

        @block.vector
        def _(dve):
            v = nc.vector
            everything = bank[0] + bank[1] + bank[2] + bank[3]

            def keep_trailing(names):
                for name in names:
                    (hi, lo), src = weight_halves[name]
                    dve.wait_ge(split_hi, SPLIT_ORDER.index(name) + 1)
                    v.tensor_tensor(lo, src, hi.bitcast(F32), ALU.subtract).then_inc(split_lo, 1)

            dve.wait_ge(weights_turned, 1)
            for b in range(2):
                v.tensor_copy(hyp_w2T[:, 2 * b:2 * b + 2, :].rearrange("p a b -> p (a b)"),
                              everything[2 + b][:]).then_inc(weights_kept, 1)
            v.tensor_copy(dif_wvT[:].rearrange("p a b -> p (a b)"), everything[6][:]).then_inc(weights_kept, 1)
            v.tensor_copy(vec_cols[:], everything[7][:, 0:VECS]).then_inc(weights_kept, 1)
            dve.wait_ge(weights_kept, KEPT)
            for h in range(HC):
                v.tensor_scalar(hyp_w2g_raw[:, h, :], hyp_w2T[:, h, :], gamma_col[:, h:h + 1], None,
                                ALU.mult).then_inc(gamma_in, 1)
            keep_trailing(TURNED_WEIGHTS)
            dve.wait_ge(consts_in, CONSTS)
            v.tensor_tensor(bk_tmp[:], bk_rows[:, 0, :], bk_rows[:, 1, :], ALU.add).then_inc(bias_summed, 1)
            dve.wait_ge(w2_averaged, 1)
            for h in range(HC):
                v.tensor_tensor(hyp_w2c_raw[:, h, :], hyp_w2g_raw[:, h, :], everything[6][:, 0:F],
                                ALU.subtract).then_inc(mean_off, 1)
            dve.wait_ge(bias_summed, 1)
            for g in range(G):
                v.tensor_tensor(bk_sum[:, g, :], bk_tmp[:], bk_rows[:, 2, :], ALU.add).then_inc(setup_done, 1)
            dve.wait_ge(shifts_made, 1)
            v.tensor_copy(hyp_shift[:], everything[7][:, 0:F]).then_inc(setup_done, 1)
            v.tensor_copy(wa_raw[:].rearrange("p a b -> p (a b)"), everything[7][:, F:F + 2 * FC]).then_inc(setup_done, 1)
            v.tensor_copy(s_part[:], everything[7][:, F + 8:F + 10]).then_inc(setup_done, 1)
            keep_trailing(LOADED_WEIGHTS)
            dve.wait_ge(setup_done, 5)
            v.tensor_tensor(s_const[:], s_part[:, 0:1], s_part[:, 1:2], ALU.add).then_inc(setup_done, 1)
            dve.wait_ge(setup_done, 6)
            keep_trailing(MADE_WEIGHTS)
            v.tensor_tensor(s_const[:], s_const[:], ab_col[:], ALU.add).then_inc(setup_done, 1)
            dve.wait_ge(setup_done, SETUP)
            dve.wait_ge(split_lo, len(SPLIT_ORDER))
            dve.wait_ge(consts_set, 3)

            def trailing(done, dst, src, hi):
                v.tensor_tensor(dst, src, hi.bitcast(F32), ALU.subtract).then_inc(done.sem, 1)

            def flat(a):
                return a[:].rearrange("p a b c -> p (a b c)") if len(a.shape) == 4 else a[:].rearrange("p a b -> p (a b)")

            def widened(g, p):
                dve.wait_ge(hyp1_ps.sem, hyp1_ps.at(p, g + 1))
                dve.wait_ge(deg_done.sem, deg_done.at(p))
                v.scalar_tensor_tensor(h_pre[:, g, :], bank[1][1 - g][:, 0:DH], deg_inv[:, g:g + 1],
                                       hyp_b1_rows[:], ALU.mult, ALU.add).then_inc(hyp1_pre.sem, 1)

            def measure(n, g, src):
                v.bn_stats(stats[n][:, g, :], src[:, g, :]).then_inc(stated[n].sem, 1)

            def average(n, p, size):
                half_mean = stats[n][:, :, 1::3]
                half_sum = stats[n][:, :, 2::3]
                dve.wait_ge(stated[n].sem, stated[n].at(p))
                v.tensor_tensor(mean_gap[n][:], half_mean[:, :, 0], half_mean[:, :, 1], ALU.subtract)\
                    .then_inc(gap_taken[n].sem, 1)
                v.scalar_tensor_tensor(square_sum[n][:], half_sum[:, :, 0], EPS * size, half_sum[:, :, 1],
                                       ALU.add, ALU.add).then_inc(gap_taken[n].sem, 1)
                dve.wait_ge(gap_taken[n].sem, gap_taken[n].at(p, 1))
                if n != "lnh":
                    v.scalar_tensor_tensor(neg_mean[n][:], mean_gap[n][:], 0.5, half_mean[:, :, 0],
                                           ALU.mult, ALU.subtract).then_inc(gap_used[n].sem, 1)
                v.scalar_tensor_tensor(gap_square[n][:], mean_gap[n][:], 0.25, mean_gap[n][:],
                                       ALU.mult, ALU.mult).then_inc(gap_used[n].sem, 1)
                dve.wait_ge(gap_used[n].sem, gap_used[n].at(p))
                v.scalar_tensor_tensor(var_eps[n][:], square_sum[n][:], 1.0 / size, gap_square[n][:],
                                       ALU.mult, ALU.add).then_inc(averaged[n].sem, 1)

            def step(t, on):
                p0, p1, p2, p3, p4 = t, t - 1, t - 2, t - 3, t - 4
                if 4 in on:
                    dve.wait_ge(hop2_sb.sem, hop2_sb.at(p4))
                    dve.wait_ge(x3_copied.sem, x3_copied.at(p4))
                    if later(p4):
                        dve.wait_ge(normed["ln3"].sem, normed["ln3"].at(p4 - 1))
                    v.scalar_tensor_tensor(flat(r3), flat(hop2), 0.0, flat(x3_kept), ALU.max, ALU.add)\
                        .then_inc(summed["ln3"].sem, 1)
                if 0 in on:
                    dve.wait_ge(ax_hi.sem, ax_hi.at(p0))
                    trailing(ax_lo, flat(axT[1]), bank[0][1][:], flat(axT[0]))
                if 1 in on:
                    dve.wait_ge(k_sb.sem, k_sb.at(p1))
                    v.tensor_scalar(deg_pos[:], deg[:, :, 1], 0.0, None, ALU.is_gt).then_inc(deg_prep.sem, 1)
                    v.tensor_scalar(deg_safe[:], deg[:, :, 1], TINY, None, ALU.max).then_inc(deg_prep.sem, 1)
                    dve.wait_ge(deg_prep.sem, deg_prep.at(p1))
                    v.reciprocal(deg_rec[:], deg_safe[:]).then_inc(deg_recip.sem, 1)
                    dve.wait_ge(deg_recip.sem, deg_recip.at(p1))
                    v.tensor_tensor(deg_inv[:], deg_rec[:], deg_pos[:], ALU.mult).then_inc(deg_done.sem, 1)
                    dve.wait_ge(deg_done.sem, deg_done.at(p1, 1))
                    v.tensor_tensor(row_sum[:], deg_inv[:], deg[:, :, 0], ALU.mult).then_inc(deg_done.sem, 1)
                    dve.wait_ge(kx_hi.sem, kx_hi.at(p1))
                    trailing(kx_lo, flat(kxT[1]), bank[1][0][:], flat(kxT[0]))
                if 4 in on:
                    dve.wait_ge(summed["ln3"].sem, summed["ln3"].at(p4))
                    for g in range(G):
                        measure("ln3", g, r3)
                    average("ln3", p4, F)
                if 3 in on:
                    dve.wait_ge(s_y2_sb.sem, s_y2_sb.at(p3))
                    v.tensor_scalar(s_col[:], s_y2[:, :, 0], s_const[:], None, ALU.add).then_inc(s_sb.sem, 1)
                    dve.wait_ge(s_sb.sem, s_sb.at(p3))
                    v.tensor_scalar(s_col02[:], s_col[:], 0.2, None, ALU.mult).then_inc(s02_sb.sem, 1)
                if 2 in on:
                    dve.wait_ge(x2T_hi.sem, x2T_hi.at(p2))
                    trailing(x2T_lo, flat(x2T[1]), bank[2][0][:], flat(x2T[0]))
                if 0 in on:
                    dve.wait_ge(adjT_sb.sem, adjT_sb.at(p0))
                    for g in range(G):
                        v.tensor_scalar(incT[:, g, :], adjT0[:, g, :], 0.0, None, ALU.not_equal, ALU.add,
                                        accum_out=edge_size[:, g:g + 1]).then_inc(inc_made.sem, 1)
                    dve.wait_ge(inc_made.sem, inc_made.at(p0))
                    v.tensor_scalar(edge_size1[:], edge_size[:], 1.0, None, ALU.max).then_inc(size_floor.sem, 1)
                    dve.wait_ge(size_floor.sem, size_floor.at(p0))
                    v.reciprocal(edge_inv[:], edge_size1[:]).then_inc(size_inv.sem, 1)
                    dve.wait_ge(size_inv.sem, size_inv.at(p0))
                    v.tensor_tensor(incT_w[:, :, N], edge_inv[:], edge_size[:], ALU.mult).then_inc(deg_rhs_set.sem, 1)
                    v.tensor_copy(incT_w[:, :, N + 1], adjT0[:, :, 0]).then_inc(deg_rhs_set.sem, 1)
                if 1 in on:
                    widened(0, p1)
                    widened(1, p1)
                    for g in range(G):
                        dve.wait_ge(relu_sb.sem, relu_sb.at(p1, g + 1))
                        measure("lnh", g, h_act)
                    average("lnh", p1, DH)
                if 2 in on:
                    dve.wait_ge(ak_ps.sem, ak_ps.at(p2))
                    for g in range(G):
                        v.scalar_tensor_tensor(qak[:, g, :], bank[2][1][:, g * DA:(g + 1) * DA], INV_SCALE,
                                               qkv[:, g, 0:DA], ALU.mult, ALU.mult,
                                               accum_out=score[:, g:g + 1]).then_inc(scored.sem, 1)
                if 3 in on:
                    dve.wait_ge(edge_exp.sem, edge_exp.at(p3))
                    if later(p3):
                        dve.wait_ge(alpha_made.sem, alpha_made.at(p3 - 1))
                    v.tensor_tensor(flat(e_max), flat(e_pos), flat(e_neg), ALU.max).then_inc(e_maxed.sem, 1)
                if 1 in on:
                    dve.wait_ge(rooted["lnh"].sem, rooted["lnh"].at(p1))
                    for g in range(G):
                        v.tensor_scalar(kmat_r[:, g, :], kmat[:, g, :], rstd["lnh"][:, g:g + 1], None,
                                        ALU.mult).then_inc(normed["lnh"].sem, 1)
                if 2 in on:
                    dve.wait_ge(score_ps.sem, score_ps.at(p2))
                    v.tensor_reduce(neg_max[:], bank[2][0][0:G, 0:N], AX.X, ALU.max, negate=True).then_inc(max_found.sem, 1)
                if 1 in on:
                    dve.wait_ge(xx_made.sem, xx_made.at(p1))
                    for g in range(G):
                        v.scalar_tensor_tensor(r1_base[:, g, :], hyp_shift[:], row_sum[:, g:g + 1], xx[:, g, :],
                                               ALU.mult, ALU.add).then_inc(r1_based.sem, 1)
                if 2 in on:
                    dve.wait_ge(prob_exp.sem, prob_exp.at(p2))
                    v.reciprocal(prob_inv[:], prob_sum[:]).then_inc(sum_inverted.sem, 1)
                    dve.wait_ge(sum_inverted.sem, sum_inverted.at(p2))
                    v.tensor_scalar(prob_row[:], prob_e[:], prob_inv[:], None, ALU.mult).then_inc(prob_normed.sem, 1)
                if 0 in on:
                    dve.wait_ge(size_inv.sem, size_inv.at(p0))
                    for g in range(G):
                        v.tensor_scalar(incT_w[:, g, 0:N], incT[:, g, :], edge_inv[:, g:g + 1], None,
                                        ALU.mult).then_inc(incw_made.sem, 1)
                if 1 in on:
                    dve.wait_ge(kz_hi.sem, kz_hi.at(p1, 1))
                    trailing(kz_lo, kzT[1][:, 0, :, :].rearrange("p h n -> p (h n)"), bank[1][1][:],
                             kzT[0][:, 0, :, :].rearrange("p h n -> p (h n)"))
                if 2 in on:
                    dve.wait_ge(prob_ps.sem, prob_ps.at(p2))
                    v.tensor_copy(prob[:], bank[2][0][:, 0:G]).then_inc(prob_sb.sem, 1)
                    dve.wait_ge(prob_sb.sem, prob_sb.at(p2))
                    for g in range(G):
                        v.scalar_tensor_tensor(r2[:, g, :], qkv[:, g, QK:QKV], prob[:, g:g + 1], x2[:, g, :],
                                               ALU.mult, ALU.add).then_inc(summed["ln2"].sem, 1)
                    for g in range(G):
                        dve.wait_ge(summed["ln2"].sem, summed["ln2"].at(p2, g + 1))
                        measure("ln2", g, r2)
                    average("ln2", p2, F)
                if 1 in on:
                    dve.wait_ge(kz_hi.sem, kz_hi.at(p1, 2))
                    trailing(kz_lo, kzT[1][:, 1, :, :].rearrange("p h n -> p (h n)"), bank[1][0][:],
                             kzT[0][:, 1, :, :].rearrange("p h n -> p (h n)"))
                if 0 in on:
                    dve.wait_ge(gcn_ps.sem, gcn_ps.at(p0))
                    dve.wait_ge(x_b3_made.sem, x_b3_made.at(p0))
                    v.tensor_tensor(flat(r0), bank[0][0][:], flat(x_b3), ALU.add).then_inc(summed["ln0"].sem, 1)
                    dve.wait_ge(summed["ln0"].sem, summed["ln0"].at(p0))
                    for g in range(G):
                        measure("ln0", g, r0)
                if 3 in on:
                    for g in range(G):
                        dve.wait_ge(hop1_ps.sem, hop1_ps.at(p3, g + 1))
                        v.tensor_scalar(sum_eps[:, g:g + 1], bank[3][g][:, F:F + 1], 1e-12, None,
                                        ALU.add).then_inc(rsum_eps.sem, 1)
                    dve.wait_ge(rsum_eps.sem, rsum_eps.at(p3))
                    v.reciprocal(sum_inv[:], sum_eps[:]).then_inc(rsum_inv.sem, 1)
                if 0 in on:
                    average("ln0", p0, F)
                if 3 in on:
                    dve.wait_ge(rsum_inv.sem, rsum_inv.at(p3))
                    for g in range(G):
                        v.scalar_tensor_tensor(hop1[:, g, :], bank[3][g][:, 0:F], sum_inv[:, g:g + 1],
                                               y01[:, g, F:2 * F], ALU.mult, ALU.add).then_inc(hop1_sb.sem, 1)
                if 1 in on:
                    dve.wait_ge(hyp2_ps.sem, hyp2_ps.at(p1))
                    dve.wait_ge(r1_based.sem, r1_based.at(p1))
                    for g in range(G):
                        v.scalar_tensor_tensor(r1[:, g, :], bank[1][0][:, g * F:(g + 1) * F], deg_inv[:, g:g + 1],
                                               r1_base[:, g, :], ALU.mult, ALU.add).then_inc(summed["ln1"].sem, 1)
                    for g in range(G):
                        dve.wait_ge(summed["ln1"].sem, summed["ln1"].at(p1, g + 1))
                        measure("ln1", g, r1)
                if 3 in on:
                    dve.wait_ge(hop2_ps.sem, hop2_ps.at(p3))
                    dve.wait_ge(y0_sb.sem, y0_sb.at(p3))
                    for g in range(G):
                        v.scalar_tensor_tensor(hop2[:, g, :], bank[3][1][:, g * F:(g + 1) * F], sum_inv[:, g:g + 1],
                                               y0[:, g, :], ALU.mult, ALU.add).then_inc(hop2_sb.sem, 1)
                if 1 in on:
                    average("ln1", p1, F)
                if 2 in on:
                    dve.wait_ge(x3T_hi.sem, x3T_hi.at(p2))
                    trailing(x3T_lo, flat(x3T[1]), bank[3][0][:], flat(x3T[0]))

            all_steps(dve, step)

        @block.gpsimd
        def _(pool):
            gp = nc.gpsimd
            gp.memset(ident[:], 0.0).then_inc(ident_zero, 1)
            pool.wait_ge(ident_zero, 1)
            gp.affine_select(out=ident[:], in_=ident[:], compare_op=ALU.not_equal, fill=1.0, base=0,
                             pattern=[[-1, P]], channel_multiplier=1).then_inc(ident_made, 1)
            gp.memset(s_y2[:, :, 2 + F:], 1.0).then_inc(consts_set, 1)
            gp.memset(neg_half[:], -0.5).then_inc(consts_set, 1)
            gp.memset(mean_rows[:], 1.0 / DH).then_inc(consts_set, 1)
            pool.wait_ge(consts_set, 3)
            pool.wait_ge(consts_in, CONSTS)

            def flat(a):
                return a[:].rearrange("p a b -> p (a b)")

            def trailing(done, pair, src):
                def whole(a):
                    return a[:].rearrange("p a b c -> p (a b c)")

                gp.tensor_tensor(whole(pair[1]), whole(src), whole(pair[0]).bitcast(F32), ALU.subtract)\
                    .then_inc(done.sem, 1)

            def root(n, p):
                pool.wait_ge(averaged[n].sem, averaged[n].at(p))
                if later(p):
                    pool.wait_ge(normed[n].sem, normed[n].at(p - 1))
                gp.tensor_tensor(rstd[n][:], var_eps[n][:], neg_half[:], ALU.pow).then_inc(rooted[n].sem, 1)
                if n != "lnh":
                    pool.wait_ge(rooted[n].sem, rooted[n].at(p))
                    gp.tensor_tensor(shift[n][:], neg_mean[n][:], rstd[n][:], ALU.mult).then_inc(shifted[n].sem, 1)

            def step(t, on):
                p0, p1, p2, p3, p4 = t, t - 1, t - 2, t - 3, t - 4
                if 1 in on:
                    pool.wait_ge(normed["ln0"].sem, normed["ln0"].at(p1))
                    if later(p1):
                        pool.wait_ge(r1_based.sem, r1_based.at(p1 - 1))
                    gp.tensor_tensor(flat(xx), flat(x1), flat(hyp_b2_rows), ALU.add).then_inc(xx_half.sem, 1)
                    pool.wait_ge(xx_half.sem, xx_half.at(p1))
                    gp.tensor_tensor(flat(xx), flat(xx), flat(x1), ALU.add).then_inc(xx_made.sem, 1)
                if 0 in on:
                    pool.wait_ge(x_loaded.sem, x_loaded.at(p0))
                    if later(p0):
                        pool.wait_ge(summed["ln0"].sem, summed["ln0"].at(p0 - 1))
                    gp.tensor_tensor(flat(x_b3), flat(x_in), flat(b3_rows), ALU.add).then_inc(x_b3_made.sem, 1)
                    pool.wait_ge(h1_hi.sem, h1_hi.at(p0))
                    trailing(h1_lo, h1T, h1T_raw)
                if 4 in on:
                    root("ln3", p4)
                if 1 in on:
                    root("lnh", p1)
                if 3 in on:
                    pool.wait_ge(e_maxed.sem, e_maxed.at(p3))
                    pool.wait_ge(adj3_kept.sem, adj3_kept.at(p3))
                    if later(p3):
                        pool.wait_ge(hop2_ps.sem, hop2_ps.at(p3 - 1))
                    for g in range(G):
                        gp.tensor_tensor(alphaT[:, g, :], e_max[:, g, :], adjT3[:, g, :],
                                         ALU.mult).then_inc(alpha_made.sem, 1)
                if 0 in on:
                    pool.wait_ge(h2_hi.sem, h2_hi.at(p0))
                    trailing(h2_lo, h2T, h2T_raw)
                if 2 in on:
                    root("ln2", p2)
                if 3 in on:
                    pool.wait_ge(y01_sb.sem, y01_sb.at(p3))
                    if later(p3):
                        pool.wait_ge(hop2_sb.sem, hop2_sb.at(p3 - 1))
                    gp.tensor_tensor(y0[:], y01[:, :, 0:F], bk_sum[:], ALU.add).then_inc(y0_sb.sem, 1)
                if 0 in on:
                    root("ln0", p0)
                if 1 in on:
                    root("ln1", p1)

            all_steps(pool, step)

    return nc


_INS = ["x", "adj", "L0_gnn_W1", "L0_gnn_b1", "L0_gnn_W2", "L0_gnn_b2", "L0_gnn_W3", "L0_gnn_b3",
        "L1_gnn_W1", "L1_gnn_b1", "L1_gnn_gamma", "L1_gnn_beta", "L1_gnn_W2", "L1_gnn_b2",
        "L2_gnn_W_qk", "L2_gnn_W_v",
        "L3_gnn_Wv", "L3_gnn_bv", "L3_gnn_aw", "L3_gnn_ab", "L3_gnn_Wk", "L3_gnn_bk"]


def kernel(**inputs):
    import numpy as np
    import concourse.bacc as bacc
    from concourse.bass_utils import run_bass_kernel_spmd

    nc = bacc.Bacc("TRN2", target_bir_lowering=False, num_devices=1)
    arrays, args = {}, []
    for name in _INS:
        a = np.ascontiguousarray(inputs[name])
        arrays[f"in_{name}"] = a
        args.append(nc.dram_tensor(f"in_{name}", a.shape, mybir.dt.from_np(a.dtype), kind="ExternalInput").ap())
    args.append(nc.dram_tensor("out", inputs["x"].shape, F32, kind="ExternalOutput").ap())
    graph_block_kernel(nc, *args)
    return run_bass_kernel_spmd(nc, [arrays], core_ids=[0]).results[0]["out"]
```
